# Optimizing a Trainium2 kernel written in Bass

```python
import numpy as np
import jax
import jax.numpy as jnp

def _softmax(x, axis=-1):
    return jax.nn.softmax(x, axis=axis)

def _gelu(x):
    return jax.nn.gelu(x, approximate=True)

def _silu(x):
    return jax.nn.silu(x)

def _sigmoid(x):
    return jax.nn.sigmoid(x)

def _layernorm(x, axis=-1, eps=1e-05):
    m = jnp.mean(x, axis=axis, keepdims=True)
    v = jnp.var(x, axis=axis, keepdims=True)
    return (x - m) / jnp.sqrt(v + eps)

def _scatter_add(tgt, idx, src, axis=0):
    return tgt.at[idx].add(src)

def _segment_sum(src, seg, n):
    return jax.ops.segment_sum(src, seg, n)
kernel_name = 'mk_xattn_seq_d2_seqx_r4_10b51a'

def setup_inputs(seed: int=0):
    np.random.seed(seed)
    _w = jnp.asarray

    def _rec_inputs():
        import jax
        import jax.numpy as jnp
        _rk = jax.random.key(seed)
        x = 7.22e-05 + 1 * jax.random.normal(jax.random.fold_in(_rk, 1), (16, 112, 512), jnp.float32)
        _lenS = 112 - jax.random.randint(jax.random.fold_in(_rk, 7), (16,), 0, max(1, 112 // 4) + 1, jnp.int32)
        _lenS2 = 375 - jax.random.randint(jax.random.fold_in(_rk, 8), (16,), 0, max(1, 375 // 4) + 1, jnp.int32)
        _ctx_2048P = jax.random.normal(jax.random.fold_in(_rk, 11), (16, 16, 512), jnp.float32)
        _ctx_2048c = jax.random.dirichlet(jax.random.fold_in(_rk, 511), 0.3 * jnp.ones((16,), jnp.float32), (16, 375))
        _ctx_2048t = jnp.einsum('bsk,bkd->bsd', _ctx_2048c, _ctx_2048P)
        _ctx_2048t = _ctx_2048t * jax.lax.rsqrt(jnp.mean(jnp.square(_ctx_2048t)) + 1e-12) * 0.953939
        ctx_2048 = 2.81802e-05 + 1.00001 * (_ctx_2048t + 0.3 * jax.random.normal(jax.random.fold_in(_rk, 611), (16, 375, 512), jnp.float32))
        _validS = jnp.arange(112)[None, :] < _lenS[:, None]
        _validS2 = jnp.arange(375)[None, :] < _lenS2[:, None]
        _causal = jnp.tril(jnp.ones((112, 112), dtype=bool))
        mask_BxS2_bf1 = jnp.ones((16, 375), dtype=bool)
        return (x, ctx_2048, mask_BxS2_bf1)
    x, ctx_2048, mask_BxS2_bf1 = _rec_inputs()

    def _L0_xattn_setup():
        import jax, jax.numpy as jnp
        import numpy as np
        D = 512
        H = 16
        HD = D // H
        INNER = 4 * D
        EPS = 1e-05

        def layer_norm(x, w, b):
            mu = jnp.mean(x, axis=-1, keepdims=True)
            var = jnp.mean(jnp.square(x - mu), axis=-1, keepdims=True)
            return (x - mu) * jax.lax.rsqrt(var + EPS) * w + b
        key = jax.random.key(seed)
        ks = jax.random.split(key, 12)
        B, LQ, LK = (4, 256, 512)
        std = 0.02
        inp = {'hidden_states': jax.random.normal(ks[0], (B, LQ, D), jnp.float32), 'encoder_hidden_states': jax.random.normal(ks[1], (B, LK, D), jnp.float32), 'encoder_attention_mask': jnp.ones((B, LK), dtype=bool), 'ln1_w': jnp.ones((D,), jnp.float32), 'ln1_b': jnp.zeros((D,), jnp.float32), 'q_w': jax.random.normal(ks[2], (D, D), jnp.float32) * std, 'q_b': jnp.zeros((D,), jnp.float32), 'k_w': jax.random.normal(ks[3], (D, D), jnp.float32) * std, 'k_b': jnp.zeros((D,), jnp.float32), 'v_w': jax.random.normal(ks[4], (D, D), jnp.float32) * std, 'v_b': jnp.zeros((D,), jnp.float32), 'cproj_w': jax.random.normal(ks[5], (D, D), jnp.float32) * std, 'cproj_b': jnp.zeros((D,), jnp.float32), 'ln2_w': jnp.ones((D,), jnp.float32), 'ln2_b': jnp.zeros((D,), jnp.float32), 'fc_w': jax.random.normal(ks[6], (D, INNER), jnp.float32) * std, 'fc_b': jnp.zeros((INNER,), jnp.float32), 'proj_w': jax.random.normal(ks[7], (INNER, D), jnp.float32) * std, 'proj_b': jnp.zeros((D,), jnp.float32)}
        return inp
    _L0_xattn_all = _L0_xattn_setup()
    _L0_xattn_in = {k: v for k, v in _L0_xattn_all.items() if k in ('ln1_w', 'ln1_b', 'q_w', 'q_b', 'k_w', 'k_b', 'v_w', 'v_b', 'cproj_w', 'cproj_b', 'ln2_w', 'ln2_b', 'fc_w', 'fc_b', 'proj_w', 'proj_b')}
    del _L0_xattn_all

    def _L1_xattn_setup():
        import jax, jax.numpy as jnp
        import numpy as np
        E, H, L, B = (512, 32, 256, 4)
        S = E // H
        DM, DD = (32, 64)

        def _ln(x, w, b, eps=1e-05):
            m = x.mean(-1, keepdims=True)
            v = ((x - m) ** 2).mean(-1, keepdims=True)
            return (x - m) / jnp.sqrt(v + eps) * w + b

        def _block(x, state, ln1_w, ln1_b, ln2_w, ln2_b, maa_x, maa_w1, maa_w2, maa_stack, time_decay, td_w1, td_w2, u, Wr, Wk, Wv, Wg, Wo, gn_w, gn_b, ffn_maa_k, ffn_maa_r, Wfk, Wfr, Wfv):
            b, l, e = x.shape
            h = u.shape[0]
            s_ = e // h
            xa = _ln(x, ln1_w, ln1_b)
            sx = jnp.concatenate([state[:, 1:2] - xa[:, :1], xa[:, :-1] - xa[:, 1:]], axis=1)
            xxx = jnp.tanh((xa + sx * maa_x) @ maa_w1).reshape(b, l, 5, DM)
            xxx = jnp.einsum('blfd,fde->blfe', xxx, maa_w2)
            xm = xa[:, :, None] + sx[:, :, None] * (maa_stack + xxx)
            xk, xw, xv, xr, xg = (xm[:, :, j] for j in range(5))
            w = jnp.exp(-jnp.exp(time_decay + jnp.tanh(xw @ td_w1) @ td_w2)).reshape(b, l, h, s_)
            r = (xr @ Wr.T).reshape(b, l, h, s_)
            k = (xk @ Wk.T).reshape(b, l, h, s_)
            v = (xv @ Wv.T).reshape(b, l, h, s_)
            g = jax.nn.silu(xg @ Wg.T)
            s0 = state[:, 2:2 + s_].reshape(b, h, s_, s_)

            def step(s, rkvw):
                r_t, k_t, v_t, w_t = rkvw
                a = k_t[..., :, None] * v_t[..., None, :]
                out = jnp.einsum('bhi,bhij->bhj', r_t, u * a + s)
                s = a + w_t[..., :, None] * s
                return (s, out)
            rkvw = tuple((jnp.moveaxis(t, 1, 0) for t in (r, k, v, w)))
            _, out = jax.lax.scan(step, s0, rkvw)
            out = jnp.moveaxis(out, 0, 1).reshape(b, l, e)
            og = out.reshape(b, l, h, s_)
            m = og.mean(-1, keepdims=True)
            va = ((og - m) ** 2).mean(-1, keepdims=True)
            og = ((og - m) / jnp.sqrt(va + 1e-05)).reshape(b, l, e) * gn_w + gn_b
            x1 = x + og * g @ Wo.T
            xc = _ln(x1, ln2_w, ln2_b)
            sx2 = jnp.concatenate([state[:, 0:1] - xc[:, :1], xc[:, :-1] - xc[:, 1:]], axis=1)
            xk2 = xc + sx2 * ffn_maa_k
            xr2 = xc + sx2 * ffn_maa_r
            rr = jax.nn.sigmoid(xr2 @ Wfr.T)
            kk = jnp.square(jax.nn.relu(xk2 @ Wfk.T))
            return x1 + rr * (kk @ Wfv.T)
        key = jax.random.key(seed)
        ks = jax.random.split(key, 24)
        sc = 0.02
        d = {'x': jax.random.normal(ks[0], (B, L, E), jnp.float32), 'state': jax.random.normal(ks[1], (B, 2 + S, E), jnp.float32) * 0.1, 'ln1_w': jnp.ones((E,), jnp.float32), 'ln1_b': jnp.zeros((E,), jnp.float32), 'ln2_w': jnp.ones((E,), jnp.float32), 'ln2_b': jnp.zeros((E,), jnp.float32), 'maa_x': jax.random.normal(ks[2], (E,), jnp.float32) * 0.1, 'maa_w1': jax.random.normal(ks[3], (E, 5 * DM), jnp.float32) * sc, 'maa_w2': jax.random.normal(ks[4], (5, DM, E), jnp.float32) * sc, 'maa_stack': jax.random.normal(ks[5], (1, 5, E), jnp.float32) * 0.1, 'time_decay': jax.random.normal(ks[6], (E,), jnp.float32) * 0.5, 'td_w1': jax.random.normal(ks[7], (E, DD), jnp.float32) * sc, 'td_w2': jax.random.normal(ks[8], (DD, E), jnp.float32) * sc, 'u': jax.random.normal(ks[9], (H, S, 1), jnp.float32) * 0.1, 'Wr': jax.random.normal(ks[10], (E, E), jnp.float32) * sc, 'Wk': jax.random.normal(ks[11], (E, E), jnp.float32) * sc, 'Wv': jax.random.normal(ks[12], (E, E), jnp.float32) * sc, 'Wg': jax.random.normal(ks[13], (E, E), jnp.float32) * sc, 'Wo': jax.random.normal(ks[14], (E, E), jnp.float32) * sc, 'gn_w': jnp.ones((E,), jnp.float32), 'gn_b': jnp.zeros((E,), jnp.float32), 'ffn_maa_k': jax.random.normal(ks[15], (E,), jnp.float32) * 0.1, 'ffn_maa_r': jax.random.normal(ks[16], (E,), jnp.float32) * 0.1, 'Wfk': jax.random.normal(ks[17], (E, E), jnp.float32) * sc, 'Wfr': jax.random.normal(ks[18], (E, E), jnp.float32) * sc, 'Wfv': jax.random.normal(ks[19], (E, E), jnp.float32) * sc}
        return d
    _L1_xattn_all = _L1_xattn_setup()
    _L1_xattn_in = {k: v for k, v in _L1_xattn_all.items() if k in ('ln1_w', 'ln1_b', 'ln2_w', 'ln2_b', 'maa_x', 'maa_w1', 'maa_w2', 'maa_stack', 'time_decay', 'td_w1', 'td_w2', 'u', 'Wr', 'Wk', 'Wv', 'Wg', 'Wo', 'gn_w', 'gn_b', 'ffn_maa_k', 'ffn_maa_r', 'Wfk', 'Wfr', 'Wfv')}
    del _L1_xattn_all
    return {'x': x, 'ctx_2048': ctx_2048, 'mask_BxS2_bf1': mask_BxS2_bf1, 'L0_xattn_ln1_w': _L0_xattn_in['ln1_w'], 'L0_xattn_ln1_b': _L0_xattn_in['ln1_b'], 'L0_xattn_q_w': _L0_xattn_in['q_w'], 'L0_xattn_q_b': _L0_xattn_in['q_b'], 'L0_xattn_k_w': _L0_xattn_in['k_w'], 'L0_xattn_k_b': _L0_xattn_in['k_b'], 'L0_xattn_v_w': _L0_xattn_in['v_w'], 'L0_xattn_v_b': _L0_xattn_in['v_b'], 'L0_xattn_cproj_w': _L0_xattn_in['cproj_w'], 'L0_xattn_cproj_b': _L0_xattn_in['cproj_b'], 'L0_xattn_ln2_w': _L0_xattn_in['ln2_w'], 'L0_xattn_ln2_b': _L0_xattn_in['ln2_b'], 'L0_xattn_fc_w': _L0_xattn_in['fc_w'], 'L0_xattn_fc_b': _L0_xattn_in['fc_b'], 'L0_xattn_proj_w': _L0_xattn_in['proj_w'], 'L0_xattn_proj_b': _L0_xattn_in['proj_b'], 'L1_xattn_ln1_w': _L1_xattn_in['ln1_w'], 'L1_xattn_ln1_b': _L1_xattn_in['ln1_b'], 'L1_xattn_ln2_w': _L1_xattn_in['ln2_w'], 'L1_xattn_ln2_b': _L1_xattn_in['ln2_b'], 'L1_xattn_maa_x': _L1_xattn_in['maa_x'], 'L1_xattn_maa_w1': _L1_xattn_in['maa_w1'], 'L1_xattn_maa_w2': _L1_xattn_in['maa_w2'], 'L1_xattn_maa_stack': _L1_xattn_in['maa_stack'], 'L1_xattn_time_decay': _L1_xattn_in['time_decay'], 'L1_xattn_td_w1': _L1_xattn_in['td_w1'], 'L1_xattn_td_w2': _L1_xattn_in['td_w2'], 'L1_xattn_u': _L1_xattn_in['u'], 'L1_xattn_Wr': _L1_xattn_in['Wr'], 'L1_xattn_Wk': _L1_xattn_in['Wk'], 'L1_xattn_Wv': _L1_xattn_in['Wv'], 'L1_xattn_Wg': _L1_xattn_in['Wg'], 'L1_xattn_Wo': _L1_xattn_in['Wo'], 'L1_xattn_gn_w': _L1_xattn_in['gn_w'], 'L1_xattn_gn_b': _L1_xattn_in['gn_b'], 'L1_xattn_ffn_maa_k': _L1_xattn_in['ffn_maa_k'], 'L1_xattn_ffn_maa_r': _L1_xattn_in['ffn_maa_r'], 'L1_xattn_Wfk': _L1_xattn_in['Wfk'], 'L1_xattn_Wfr': _L1_xattn_in['Wfr'], 'L1_xattn_Wfv': _L1_xattn_in['Wfv']}

def reference(x, ctx_2048, mask_BxS2_bf1, L0_xattn_ln1_w, L0_xattn_ln1_b, L0_xattn_q_w, L0_xattn_q_b, L0_xattn_k_w, L0_xattn_k_b, L0_xattn_v_w, L0_xattn_v_b, L0_xattn_cproj_w, L0_xattn_cproj_b, L0_xattn_ln2_w, L0_xattn_ln2_b, L0_xattn_fc_w, L0_xattn_fc_b, L0_xattn_proj_w, L0_xattn_proj_b, L1_xattn_ln1_w, L1_xattn_ln1_b, L1_xattn_ln2_w, L1_xattn_ln2_b, L1_xattn_maa_x, L1_xattn_maa_w1, L1_xattn_maa_w2, L1_xattn_maa_stack, L1_xattn_time_decay, L1_xattn_td_w1, L1_xattn_td_w2, L1_xattn_u, L1_xattn_Wr, L1_xattn_Wk, L1_xattn_Wv, L1_xattn_Wg, L1_xattn_Wo, L1_xattn_gn_w, L1_xattn_gn_b, L1_xattn_ffn_maa_k, L1_xattn_ffn_maa_r, L1_xattn_Wfk, L1_xattn_Wfr, L1_xattn_Wfv):
    import jax
    import jax.numpy as jnp

    def _L0_xattn_ref(hidden_states, encoder_hidden_states, encoder_attention_mask, ln1_w, ln1_b, q_w, q_b, k_w, k_b, v_w, v_b, cproj_w, cproj_b, ln2_w, ln2_b, fc_w, fc_b, proj_w, proj_b):
        import jax, jax.numpy as jnp
        import numpy as np
        D = 512
        H = 16
        HD = D // H
        INNER = 4 * D
        EPS = 1e-05

        def layer_norm(x, w, b):
            mu = jnp.mean(x, axis=-1, keepdims=True)
            var = jnp.mean(jnp.square(x - mu), axis=-1, keepdims=True)
            return (x - mu) * jax.lax.rsqrt(var + EPS) * w + b
        B, LQ, _ = hidden_states.shape
        LK = encoder_hidden_states.shape[1]
        residual = hidden_states
        x = layer_norm(hidden_states, ln1_w, ln1_b)
        q = (x @ q_w + q_b).reshape(B, LQ, H, HD).transpose(0, 2, 1, 3)
        k = (encoder_hidden_states @ k_w + k_b).reshape(B, LK, H, HD).transpose(0, 2, 1, 3)
        v = (encoder_hidden_states @ v_w + v_b).reshape(B, LK, H, HD).transpose(0, 2, 1, 3)
        scale = 1.0 / np.sqrt(HD).astype(np.float32)
        scores = jnp.einsum('bhqd,bhkd->bhqk', q, k) * scale
        mask = encoder_attention_mask[:, None, None, :]
        mask_value = jnp.finfo(scores.dtype).min
        scores = jnp.where(mask, scores, mask_value)
        attn = jax.nn.softmax(scores, axis=-1)
        out = jnp.einsum('bhqk,bhkd->bhqd', attn, v)
        out = out.transpose(0, 2, 1, 3).reshape(B, LQ, D)
        out = out @ cproj_w + cproj_b
        hidden = out + residual
        residual = hidden
        y = layer_norm(hidden, ln2_w, ln2_b)
        y = jax.nn.gelu(y @ fc_w + fc_b, approximate=True)
        y = y @ proj_w + proj_b
        return residual + y

    def _L1_xattn_ref(x, state, ln1_w, ln1_b, ln2_w, ln2_b, maa_x, maa_w1, maa_w2, maa_stack, time_decay, td_w1, td_w2, u, Wr, Wk, Wv, Wg, Wo, gn_w, gn_b, ffn_maa_k, ffn_maa_r, Wfk, Wfr, Wfv):
        import jax, jax.numpy as jnp
        import numpy as np
        E, H, L, B = (512, 32, 256, 4)
        S = E // H
        DM, DD = (32, 64)

        def _ln(x, w, b, eps=1e-05):
            m = x.mean(-1, keepdims=True)
            v = ((x - m) ** 2).mean(-1, keepdims=True)
            return (x - m) / jnp.sqrt(v + eps) * w + b

        def _block(x, state, ln1_w, ln1_b, ln2_w, ln2_b, maa_x, maa_w1, maa_w2, maa_stack, time_decay, td_w1, td_w2, u, Wr, Wk, Wv, Wg, Wo, gn_w, gn_b, ffn_maa_k, ffn_maa_r, Wfk, Wfr, Wfv):
            b, l, e = x.shape
            h = u.shape[0]
            s_ = e // h
            xa = _ln(x, ln1_w, ln1_b)
            sx = jnp.concatenate([state[:, 1:2] - xa[:, :1], xa[:, :-1] - xa[:, 1:]], axis=1)
            xxx = jnp.tanh((xa + sx * maa_x) @ maa_w1).reshape(b, l, 5, DM)
            xxx = jnp.einsum('blfd,fde->blfe', xxx, maa_w2)
            xm = xa[:, :, None] + sx[:, :, None] * (maa_stack + xxx)
            xk, xw, xv, xr, xg = (xm[:, :, j] for j in range(5))
            w = jnp.exp(-jnp.exp(time_decay + jnp.tanh(xw @ td_w1) @ td_w2)).reshape(b, l, h, s_)
            r = (xr @ Wr.T).reshape(b, l, h, s_)
            k = (xk @ Wk.T).reshape(b, l, h, s_)
            v = (xv @ Wv.T).reshape(b, l, h, s_)
            g = jax.nn.silu(xg @ Wg.T)
            s0 = state[:, 2:2 + s_].reshape(b, h, s_, s_)

            def step(s, rkvw):
                r_t, k_t, v_t, w_t = rkvw
                a = k_t[..., :, None] * v_t[..., None, :]
                out = jnp.einsum('bhi,bhij->bhj', r_t, u * a + s)
                s = a + w_t[..., :, None] * s
                return (s, out)
            rkvw = tuple((jnp.moveaxis(t, 1, 0) for t in (r, k, v, w)))
            _, out = jax.lax.scan(step, s0, rkvw)
            out = jnp.moveaxis(out, 0, 1).reshape(b, l, e)
            og = out.reshape(b, l, h, s_)
            m = og.mean(-1, keepdims=True)
            va = ((og - m) ** 2).mean(-1, keepdims=True)
            og = ((og - m) / jnp.sqrt(va + 1e-05)).reshape(b, l, e) * gn_w + gn_b
            x1 = x + og * g @ Wo.T
            xc = _ln(x1, ln2_w, ln2_b)
            sx2 = jnp.concatenate([state[:, 0:1] - xc[:, :1], xc[:, :-1] - xc[:, 1:]], axis=1)
            xk2 = xc + sx2 * ffn_maa_k
            xr2 = xc + sx2 * ffn_maa_r
            rr = jax.nn.sigmoid(xr2 @ Wfr.T)
            kk = jnp.square(jax.nn.relu(xk2 @ Wfk.T))
            return x1 + rr * (kk @ Wfv.T)
        return _block(x, state, ln1_w, ln1_b, ln2_w, ln2_b, maa_x, maa_w1, maa_w2, maa_stack, time_decay, td_w1, td_w2, u, Wr, Wk, Wv, Wg, Wo, gn_w, gn_b, ffn_maa_k, ffn_maa_r, Wfk, Wfr, Wfv)
    x = _L0_xattn_ref(x, ctx_2048, mask_BxS2_bf1, L0_xattn_ln1_w, L0_xattn_ln1_b, L0_xattn_q_w, L0_xattn_q_b, L0_xattn_k_w, L0_xattn_k_b, L0_xattn_v_w, L0_xattn_v_b, L0_xattn_cproj_w, L0_xattn_cproj_b, L0_xattn_ln2_w, L0_xattn_ln2_b, L0_xattn_fc_w, L0_xattn_fc_b, L0_xattn_proj_w, L0_xattn_proj_b)
    x = _L1_xattn_ref(x, ctx_2048, L1_xattn_ln1_w, L1_xattn_ln1_b, L1_xattn_ln2_w, L1_xattn_ln2_b, L1_xattn_maa_x, L1_xattn_maa_w1, L1_xattn_maa_w2, L1_xattn_maa_stack, L1_xattn_time_decay, L1_xattn_td_w1, L1_xattn_td_w2, L1_xattn_u, L1_xattn_Wr, L1_xattn_Wk, L1_xattn_Wv, L1_xattn_Wg, L1_xattn_Wo, L1_xattn_gn_w, L1_xattn_gn_b, L1_xattn_ffn_maa_k, L1_xattn_ffn_maa_r, L1_xattn_Wfk, L1_xattn_Wfr, L1_xattn_Wfv)
    return x

_drawn_inputs = setup_inputs


def setup_inputs(seed=0):
    import zlib

    import numpy as np

    out = dict(_drawn_inputs(seed))
    spreads = {'L0_xattn_ln1_w': (1.0, 0.6),
     'L0_xattn_ln1_b': (0.0, 0.8),
     'L0_xattn_q_b': (0.0, 0.8),
     'L0_xattn_k_b': (0.0, 0.8),
     'L0_xattn_v_b': (0.0, 0.1),
     'L0_xattn_cproj_b': (0.0, 0.1),
     'L0_xattn_ln2_w': (1.0, 0.2),
     'L0_xattn_ln2_b': (0.0, 0.328),
     'L0_xattn_fc_b': (0.0, 0.1),
     'L0_xattn_proj_b': (0.0, 0.1),
     'L1_xattn_ln1_w': (1.0, 0.2),
     'L1_xattn_ln1_b': (0.0, 0.282),
     'L1_xattn_ln2_w': (1.0, 0.6),
     'L1_xattn_ln2_b': (0.0, 0.8),
     'L1_xattn_gn_w': (1.0, 0.6),
     'L1_xattn_gn_b': (0.0, 0.727)}
    factors = {'L0_xattn_q_w': 7.1,
     'L0_xattn_k_w': 6.965,
     'L1_xattn_maa_x': 8.0,
     'L1_xattn_maa_w1': 3.105,
     'L1_xattn_maa_w2': 3.12,
     'L1_xattn_td_w1': 8.0,
     'L1_xattn_td_w2': 8.0,
     'L1_xattn_u': 3.185,
     'L1_xattn_ffn_maa_k': 6.063,
     'L1_xattn_ffn_maa_r': 8.0,
     'L1_xattn_Wfr': 4.312}
    for name, (base, spread) in spreads.items():
        noise = np.random.default_rng([zlib.crc32(name.encode()), seed]).standard_normal(out[name].shape)
        drawn = base * np.exp(spread * noise) if base else spread * noise
        out[name] = jnp.asarray(drawn.astype(out[name].dtype))
    for name, factor in factors.items():
        out[name] = (out[name] * factor).astype(out[name].dtype)
    return out
```

```python
import numpy as np
import concourse.bass as bass
import concourse.mybir as mybir
from contextlib import ExitStack

F32 = mybir.dt.float32
U8 = mybir.dt.uint8
ALU = mybir.AluOpType
ACT = mybir.ActivationFunctionType
AX = mybir.AxisListType

B, LQ, LK, D = 16, 112, 375, 512
P = 128
E = D // P
H, HD = 16, 32
INNER = 4 * D
GB = 4
NG = B // GB
T = GB * LQ
KC = 3
KW = LK // KC
RH, RS = 32, 16
JH = 8
DM, DD = 32, 64
EPS = 1e-5
SCALE = float(np.float32(1.0) / np.sqrt(np.float32(HD)))
BIG = float(2.0 ** 126)
SLOTS = 4
PIECES = 16

COLS = ["ln1_w", "ln1_b", "q_b", "k_b", "v_b", "ln2_w", "ln2_b",
        "r_ln1_w", "r_ln1_b", "r_ln2_w", "r_ln2_b", "maa_x",
        "maa_0", "maa_1", "maa_2", "maa_3", "maa_4", "decay", "gn_w", "gn_b", "mix_k", "mix_r"]
FCB = E * len(COLS)
NCOL = FCB + INNER // P
ORDER = [1, 0, 2, 3, 4]

TK, TV, TX, TQ, TO, TC, TY = 0, 4, 7, 8, 9, 10, 11
SEQ_TILES = 12
G_FC, G_LN1, G_W1, G_LOW, G_OUT, G_LN2, G_FK, G_FRV = 0, 16, 20, 21, 62, 66, 70, 74
X_AT = [21, 25, 34, 42, 50]
TD1, TD2 = 29, 30
P_AT = [None, 38, 46, 54, 58]
GROUP_OWN = 82
GROUP_TILES = GB * SEQ_TILES + GROUP_OWN
READY0 = 8

LN_GROUP = 16


class Chain:

    def __init__(self, engine, sem):
        self.engine, self.sem, self.base, self.count = engine, sem, 0, 0

    def start(self, base):
        self.base, self.count = base, 0

    def step(self, instruction):
        self.count += 1
        instruction.then_inc(self.sem, 1)

    def settle(self):
        self.engine.wait_ge(self.sem, self.base + self.count)

    def end(self, count):
        assert self.count == count, (self.count, count)


def build(nc, x, ctxT, ctx, mask, shiftcols, cols, wq, wk, wv, wc, cproj_b, proj_b, stream,
          maa_w1, maa_w2, td_w1, td_w2, u, out):
    rkw_d = nc.dram_tensor("rkw_scratch", (B * RH, RS, 3, LQ), F32, kind="Internal").ap()
    v_d = nc.dram_tensor("v_scratch", (B * RH, RS * LQ), F32, kind="Internal").ap()
    y_d = nc.dram_tensor("y_scratch", (B * RH, RS * LQ), F32, kind="Internal").ap()

    ctxm = ExitStack()
    with ctxm:
        def sb(name, shape, dt=F32):
            return ctxm.enter_context(nc.sbuf_tensor(name, shape, dt))

        def sem(name):
            return ctxm.enter_context(nc.semaphore(name))

        ident = sb("ident", [P, P])
        colt = sb("colt", [P, NCOL])
        Wq, Wk, Wv, Wc = (sb(n, [P, E, D]) for n in ("Wq", "Wk", "Wv", "Wc"))
        ring = sb("ring", [P, SLOTS, E, D])
        mw1 = sb("mw1", [P, E, 5 * DM])
        mw2 = sb("mw2", [P, D])
        mw2b = sb("mw2b", [DM, D])
        tw1 = sb("tw1", [P, E, DD])
        tw2 = sb("tw2", [DD, D])
        cb = sb("cb", [LQ, D])
        pb = sb("pb", [LQ, D])
        shc = sb("shc", [P, 2, E, B])
        ucol = sb("ucol", [P, RS])
        half = sb("half", [P, 1 + LQ])
        ctx_t = sb("ctx_t", [P, E, LK])
        x_t = sb("x_t", [LQ, D])
        res = sb("res", [LQ, D])
        xn = sb("xn", [LQ, 2, D])
        xnT = sb("xnT", [P, E, LQ])
        qT = sb("qT", [P, E, LQ])
        KT = sb("KT", [P, E, LK])
        V = sb("V", [KW, KC, H, HD + 1])
        mrow = sb("mrow", [LQ, LK], U8)
        maskb = sb("maskb", [LQ, LK])
        sm = sb("sm", [LQ, 2, LK])
        nm = sb("nm", [LQ, 2])
        prob = sb("prob", [LQ, 2, LK])
        probT = sb("probT", [KW, 2, KC * LQ])
        rden = sb("rden", [LQ, H])
        on = sb("on", [LQ, D])
        onT = sb("onT", [P, E, LQ])
        bst = sb("bst", [LQ, 6])
        mv = sb("mv", [LQ, 2])
        vare = sb("vare", [LQ, 1])
        rstd = sb("rstd", [LQ, 1])
        X = sb("X", [LQ, GB, D])
        XA = sb("XA", [P, E, GB, LQ + 1])
        SX = sb("SX", [P, E * GB, LQ])
        C = [sb("C0", [P, E, T]), sb("C1", [P, E, T])]
        HT = sb("HT", [P, E, T])
        GT = sb("GT", [P, E, T])
        TA = sb("TA", [P, T])
        TB = sb("TB", [DM, T])
        VB = sb("VB", [P, RS, LQ])
        YB = sb("YB", [P, RS, LQ])
        S = sb("S", [P, JH, LQ])
        wrep = sb("wrep", [P, 2, JH, LQ])
        rkw = sb("rkw", [P, 2, 3, LQ])
        s0 = sb("s0", [P, RS, RS])
        bon = sb("bon", [P, 2, LQ])
        gst = sb("gst", [P, 3, LQ])

        YT = SX[:, :, :].rearrange("p (e b) t -> p e (b t)", e=E)
        TD = GT[0:DD, 0, :]
        RR = [GT[0:LQ, :, :].rearrange("p e t -> p (e t)")[:, k * D:(k + 1) * D] for k in range(2)]
        XAs = XA[:, :, :, 1:LQ + 1]
        XAc = XA[:, :, :, :].rearrange("p e b t -> p (e b) t")

        bank = [ctxm.enter_context(nc.psum_tensor(f"bank{k}", [P, 512], F32)) for k in range(8)]
        dense = bank[0:2]
        score = bank[2:4]
        pT = bank[4:6]
        obank = bank[6:8]

        def col(name, e):
            k = COLS.index(name) * E + e
            return colt[:, k:k + 1]

        def colb(name, n):
            k = COLS.index(name) * E
            return colt[:, k:k + E].unsqueeze(2).to_broadcast([P, E, n])

        params_in = sem("params_in")
        consts_made = sem("consts_made")
        ring_in = [sem(f"ring_in{k}") for k in range(SLOTS)]
        ring_used = [sem(f"ring_used{k}") for k in range(SLOTS)]
        x_in = sem("x_in")
        ctx_in = sem("ctx_in")
        mask_in = sem("mask_in")
        res_ready = sem("res_ready")
        maskb_ready = sem("maskb_ready")
        var_ready = sem("var_ready")
        rstd_ready = sem("rstd_ready")
        xn_ready = sem("xn_ready")
        dense_ready = sem("dense_ready")
        dense_free = [sem("dense_free0"), sem("dense_free1")]
        score_ready = sem("score_ready")
        sm_ready = sem("sm_ready")
        prob_ready = sem("prob_ready")
        pT_ready = sem("pT_ready")
        probT_ready = sem("probT_ready")
        pv_ready = sem("pv_ready")
        on_ready = sem("on_ready")
        mlp_used = sem("mlp_used")
        acc_ready = sem("acc_ready")
        mix_ready = sem("mix_ready")
        decay_ready = sem("decay_ready")
        e_out = [sem(f"e_out{k}") for k in range(E)]
        v_in = sem("v_in")
        rkw_in = [sem("rkw_in0"), sem("rkw_in1")]
        wrep_ready = sem("wrep_ready")
        scan_step = sem("scan_step")
        y_norm = sem("y_norm")
        y_out = sem("y_out")
        y_in = sem("y_in")
        kk_ready = sem("kk_ready")
        out_ready = sem("out_ready")
        out_done = sem("out_done")
        dve_step = sem("dve_step")
        pool_step = sem("pool_step")
        carried = sem("carried")

        def tile_seq(g, b):
            return g * GROUP_TILES + b * SEQ_TILES

        def tile_group(g):
            return g * GROUP_TILES + GB * SEQ_TILES

        HALFG = GROUP_TILES // 2

        def ready(eng, half_base, k):
            eng.wait_ge(dense_ready, 2 * half_base + (READY0 + k + 1))

        def evacuated(eng, half_base, k):
            eng.wait_ge(dense_free[k % 2], half_base + (k // 2 + 2))

        def bank_free(eng, half_base, k):
            eng.wait_ge(dense_free[k % 2], half_base + (k // 2 + 1))

        def hb_seq(g, b):
            return g * HALFG + b * (SEQ_TILES // 2)

        def hb_group(g):
            return g * HALFG + GB * SEQ_TILES // 2

        PARAMS = 14

        def apart(eng):
            eng.sem_inc(carried, 1)

        block = ctxm.enter_context(nc.Block())

        @block.sync
        def _(sp):
            sp.dma_start(colt[:, :], cols).then_inc(params_in, 16)
            for dst, src in ((Wk, wk), (Wv, wv), (Wq, wq), (Wc, wc)):
                sp.dma_start(dst[:, :, :], src.rearrange("(c p) n -> p c n", p=P)).then_inc(params_in, 16)
            sp.dma_start(cb[:, :], cproj_b.partition_broadcast(LQ)).then_inc(params_in, 16)
            sp.dma_start(pb[:, :], proj_b.partition_broadcast(LQ)).then_inc(params_in, 16)
            sp.dma_start(mw1[:, :, :], maa_w1.rearrange("(c p) n -> p c n", p=P)).then_inc(params_in, 16)
            sp.dma_start(mw2[:, :], maa_w2[0:P, :]).then_inc(params_in, 16)
            sp.dma_start(mw2b[:, :], maa_w2[P:5 * DM, :]).then_inc(params_in, 16)
            sp.dma_start(tw1[:, :, :], td_w1.rearrange("(c p) n -> p c n", p=P)).then_inc(params_in, 16)
            sp.dma_start(tw2[:, :], td_w2).then_inc(params_in, 16)
            sp.dma_start(shc[:, :, :, :], shiftcols).then_inc(params_in, 16)
            sp.dma_start(ucol[:, :], u).then_inc(params_in, 16)
            sp.sem_inc(out_done, 16)

            def piece(g, k):
                sp.wait_ge(ring_used[k % SLOTS], g * (PIECES // SLOTS) + (k // SLOTS + 1))
                sp.dma_start(ring[:, k % SLOTS, :, :],
                             stream[k].rearrange("(c p) n -> p c n", p=P)).then_inc(ring_in[k % SLOTS], 16)

            with sp.Fori(0, NG) as g:
                for k in range(12):
                    piece(g, k)
                for e in range(E):
                    sp.wait_ge(e_out[e], g * 64 + 64)
                sp.dma_start(VB[:, :, :].rearrange("p j t -> p (j t)"),
                             v_d[bass.ds(g * P, P), :]).then_inc(v_in, 16)
                for b in range(GB):
                    sp.dma_start(s0[RH * b:RH * (b + 1), :, :].rearrange("p i j -> p (i j)"),
                                 ctx[g * GB + b, 2:2 + RS, :].rearrange("s (q c) -> (s q) c", c=RS * RS)
                                 ).then_inc(v_in, 16)

                def load_rkw(i, par):
                    sp.dma_start(rkw[:, par, :, :], rkw_d[bass.ds(g * P, P), i, :, :]).then_inc(rkw_in[par], 16)

                load_rkw(0, 0)
                load_rkw(1, 1)
                with sp.Fori(1, RS // 2) as ip:
                    for par in range(2):
                        sp.wait_ge(scan_step, g * RS + (ip * 2 + (par - 1)))
                        load_rkw(ip * 2 + par, par)
                for k in range(12, PIECES):
                    piece(g, k)
                sp.wait_ge(y_norm, g + 1)
                sp.dma_start(y_d[bass.ds(g * P, P), :], YB[:, :, :].rearrange("p j t -> p (j t)")).then_inc(y_out, 16)
                sp.wait_ge(y_out, g * 16 + 16)
                ready(sp, hb_group(g), P_AT[4] + 3)
                for b in range(GB):
                    sp.dma_start(C[0][:, :, b * LQ:(b + 1) * LQ],
                                 y_d[bass.ds(g * P + RH * b, RH), :].rearrange("h (j t) -> (h j) t", t=LQ)
                                 .rearrange("(e p) t -> p e t", p=P)).then_inc(y_in, 16)
                for b in range(GB):
                    sp.wait_ge(out_ready, g * GB + (b + 1))
                    sp.dma_start(out[g * GB + b, :, :], X[:, b, :]).then_inc(out_done, 16)
            sp.wait_ge(out_done, 16 * (B + 1))

        @block.gpsimd
        def _(pool):
            chain = Chain(pool, pool_step)
            chain.step(nc.gpsimd.memset(ident[:, :], 0.0))
            chain.step(nc.gpsimd.memset(half[:, :], -0.5))
            chain.step(nc.gpsimd.memset(wrep[:, :, :, :], 0.0))
            chain.step(nc.gpsimd.memset(V[:, :, :, HD:HD + 1], 1.0))
            chain.settle()
            nc.gpsimd.affine_select(out=ident[:, :], in_=ident[:, :], compare_op=ALU.not_equal, fill=1.0,
                                    base=0, pattern=[[-1, P]], channel_multiplier=1).then_inc(consts_made, 1)
            pool.sem_inc(xn_ready, 2)
            pool.wait_ge(params_in, 16 * PARAMS)
            POOL_SEQ, POOL_GROUP = 2, 9
            START = 4

            def inv_std(count, rows=None, var=None, res_ap=None, scale=1.0):
                pool.wait_ge(var_ready, count)
                apart(pool)
                n = 1 if var is None else LQ
                src = mv[:, 1:2] if var is None else var
                tmp = vare[:, :] if var is None else res_ap
                dst = rstd[:, :] if var is None else res_ap
                chain.step(nc.gpsimd.tensor_scalar(tmp, src, scale, EPS, ALU.mult, ALU.add))
                chain.settle()
                rows = LQ if var is None else P
                nc.gpsimd.tensor_tensor(dst, tmp, half[0:rows, 0:n], ALU.pow).then_inc(rstd_ready, 1)

            POOL_ALL = GB * POOL_SEQ + POOL_GROUP
            with pool.Fori(0, NG) as g:
                with pool.Fori(0, GB) as b:
                    n = g * GB + b
                    chain.start(g * POOL_ALL + b * POOL_SEQ + START)
                    hb = hb_seq(g, b)
                    pool.wait_ge(xn_ready, g * LN_GROUP + b * 2 + 1)
                    pool.dma_start(x_t[:, :], x[n, :, :]).then_inc(x_in, 16)
                    pool.wait_ge(dense_ready, 2 * hb + (READY0 - SEQ_TILES + TV + KC))
                    pool.dma_start(ctx_t[:, :, :], ctxT[n, :, :].rearrange("(c p) t -> p c t", p=P)).then_inc(ctx_in, 16)
                    pool.dma_start(mrow[:, :], mask[n, :].partition_broadcast(LQ)).then_inc(mask_in, 16)
                    inv_std(g * (LN_GROUP + 1) + b * 2 + 1)
                    pool.wait_ge(dense_free[0], hb + 1)
                    nc.gpsimd.tensor_tensor(res[:, :], x_t[:, :], cb[:, :], ALU.add).then_inc(res_ready, 1)
                    pool.wait_ge(mask_in, n * 16 + 16)
                    apart(pool)
                    nc.gpsimd.tensor_scalar(maskb[:, :], mrow[:, :], BIG, -BIG, ALU.mult, ALU.add).then_inc(maskb_ready, 1)
                    inv_std(g * (LN_GROUP + 1) + b * 2 + 2)
                    chain.end(POOL_SEQ)
                chain.start(g * POOL_ALL + GB * POOL_SEQ + START)
                hb = hb_group(g)
                for b in range(GB):
                    inv_std(g * (LN_GROUP + 1) + (9 + b))

                def store(which, e):
                    rows = bass.ds(g * P, P)
                    if which == 3:
                        dst = v_d[rows, :].rearrange("(b h) (j t) -> b (h j) t", b=GB, t=LQ)[:, e * P:(e + 1) * P, :]
                    else:
                        dst = rkw_d[rows, :, :, :].rearrange("(b h) i s t -> b (h i) s t", b=GB)[
                            :, e * P:(e + 1) * P, which, :]
                    pool.dma_start(dst.rearrange("b p t -> p b t"),
                                   HT[:, e, :].rearrange("p (b t) -> p b t", b=GB)).then_inc(e_out[e], 16)

                for e in range(E):
                    pool.wait_ge(decay_ready, g * E + (e + 1))
                    store(2, e)
                for j, which in ((1, 1), (2, 3), (3, 0)):
                    for e in range(E):
                        evacuated(pool, hb, P_AT[j] + e)
                        store(which, e)

                def repeat_decay(par, count):
                    pool.wait_ge(rkw_in[par], count)
                    apart(pool)
                    nc.gpsimd.tensor_copy(wrep[:, par, :, 1:LQ],
                                          rkw[:, par, 2, 0:LQ - 1].unsqueeze(1).to_broadcast([P, JH, LQ - 1])
                                          ).then_inc(wrep_ready, 1)

                with pool.Fori(0, RS // 2) as ip:
                    for par in range(2):
                        repeat_decay(par, g * 128 + ip * 16 + 16)
                inv_std(g * (LN_GROUP + 1) + 13, var=gst[:, 1, :], res_ap=gst[:, 2, :], scale=1.0 / RS)
                for b in range(GB):
                    inv_std(g * (LN_GROUP + 1) + (14 + b))
                chain.end(POOL_GROUP)

        @block.scalar
        def _(act):
            act.sem_inc(dense_free[0], 1)
            act.sem_inc(dense_free[1], 1)
            act.wait_ge(params_in, 16 * PARAMS)

            def copy_cols(dst, psum, w, bcol, e):
                return nc.scalar.activation(dst, psum, ACT.Identity, bias=col(bcol, e), scale=col(w, e))

            with act.Fori(0, NG) as g:
                with act.Fori(0, GB) as b:
                    n = g * GB + b
                    hb = hb_seq(g, b)
                    for e in range(E):
                        ready(act, hb, TK + e)
                        nc.scalar.activation(KT[:, e, :], dense[(TK + e) % 2][:, 0:LK], ACT.Identity,
                                             bias=col("k_b", e)).then_inc(dense_free[(TK + e) % 2], 1)
                    for k in range(KC):
                        ready(act, hb, TV + k)
                        nc.scalar.activation(V[:, k, :, 0:HD],
                                             dense[(TV + k) % 2][0:KW, :].rearrange("p (h d) -> p h d", h=H),
                                             ACT.Copy).then_inc(dense_free[(TV + k) % 2], 1)
                    ready(act, hb, TX)
                    for e in range(E):
                        last = copy_cols(xnT[:, e, :], dense[TX % 2][:, e * LQ:(e + 1) * LQ], "ln1_w", "ln1_b", e)
                    last.then_inc(dense_free[TX % 2], 1)

                    def move_pT(u):
                        act.wait_ge(pT_ready, n * H + (u + 1))
                        if u >= 2:
                            act.wait_ge(pv_ready, n * H + (u - 1))
                        nc.scalar.activation(probT[:, u % 2, :], pT[u % 2][0:KW, 0:KC * LQ],
                                             ACT.Copy).then_inc(probT_ready, 1)

                    for u in range(H):
                        act.wait_ge(sm_ready, n * H + (u + 1))
                        if u >= 2:
                            act.wait_ge(pT_ready, n * H + (u - 1))
                        nc.scalar.activation(prob[:, u % 2, :], sm[:, u % 2, :], ACT.Exp,
                                             bias=nm[:, u % 2:u % 2 + 1], scale=-1.0).then_inc(prob_ready, 1)
                        if u >= 1:
                            move_pT(u - 1)
                    move_pT(H - 1)
                    ready(act, hb, TY)
                    for e in range(E):
                        last = copy_cols(YT[:, e, bass.ds(b * LQ, LQ)], dense[TY % 2][:, e * LQ:(e + 1) * LQ],
                                         "ln2_w", "ln2_b", e)
                    last.then_inc(dense_free[TY % 2], 1)

                hb = hb_group(g)
                for m in range(4):
                    if m >= 1:
                        act.wait_ge(mlp_used, g * 4 + m)
                    for e in range(E):
                        k = G_FC + 4 * m + e
                        ready(act, hb, k)
                        nc.scalar.activation(HT[:, e, :], dense[k % 2][:, 0:T], ACT.Gelu_apprx_tanh,
                                             bias=colt[:, FCB + 4 * m + e:FCB + 4 * m + e + 1]
                                             ).then_inc(dense_free[k % 2], 1)

                def ln_cols(first, w, bcol):
                    for b in range(GB):
                        k = first + b
                        ready(act, hb, k)
                        for e in range(E):
                            last = copy_cols(XA[:, e, b, 1:LQ + 1], dense[k % 2][:, e * LQ:(e + 1) * LQ], w, bcol, e)
                        last.then_inc(dense_free[k % 2], 1)

                ln_cols(G_LN1, "r_ln1_w", "r_ln1_b")
                ready(act, hb, G_W1)
                nc.scalar.activation(TA[:, :], dense[G_W1 % 2][:, 0:T], ACT.Tanh)
                nc.scalar.activation(TB[:, :], score[0][0:DM, 0:T], ACT.Tanh).then_inc(dense_free[G_W1 % 2], 1)
                ready(act, hb, TD1)
                nc.scalar.activation(TD, dense[TD1 % 2][0:DD, 0:T], ACT.Tanh).then_inc(dense_free[TD1 % 2], 1)
                for e in range(E):
                    k = TD2 + e
                    ready(act, hb, k)
                    nc.scalar.activation(HT[:, e, :], dense[k % 2][:, 0:T], ACT.Exp,
                                         bias=col("decay", e)).then_inc(dense_free[k % 2], 1)
                for e in range(E):
                    evacuated(act, hb, TD2 + e)
                    nc.scalar.activation(HT[:, e, :], HT[:, e, :], ACT.Exp, scale=-1.0).then_inc(decay_ready, 1)
                for j in (1, 2, 3):
                    for e in range(E):
                        k = P_AT[j] + e
                        ready(act, hb, k)
                        act.wait_ge(e_out[e], g * 64 + 16 * j)
                        nc.scalar.activation(HT[:, e, :], dense[k % 2][:, 0:T],
                                             ACT.Copy).then_inc(dense_free[k % 2], 1)
                for e in range(E):
                    k = P_AT[4] + e
                    ready(act, hb, k)
                    nc.scalar.activation(GT[:, e, :], dense[k % 2][:, 0:T], ACT.Silu).then_inc(dense_free[k % 2], 1)
                ln_cols(G_LN2, "r_ln2_w", "r_ln2_b")
                for e in range(E):
                    k = G_FK + e
                    ready(act, hb, k)
                    act.wait_ge(e_out[e], g * 64 + 64)
                    nc.scalar.activation(HT[:, e, :], dense[k % 2][:, 0:T], ACT.Relu).then_inc(dense_free[k % 2], 1)
                for e in range(E):
                    evacuated(act, hb, G_FK + e)
                    nc.scalar.activation(HT[:, e, :], HT[:, e, :], ACT.Square).then_inc(kk_ready, 1)
                for b in range(GB):
                    k = G_FRV + 2 * b
                    ready(act, hb, k)
                    if b >= 2:
                        evacuated(act, hb, k - 3)
                    nc.scalar.activation(RR[b % 2], dense[k % 2][0:LQ, :], ACT.Sigmoid).then_inc(dense_free[k % 2], 1)

        @block.vector
        def _(dve):
            chain = Chain(dve, dve_step)
            DVE_SEQ, DVE_PRE, DVE_PAIR, DVE_MID, DVE_POST = 4, 13, 22, 6, 8
            DVE_GROUP = DVE_PRE + DVE_PAIR * (RS // 2) + DVE_MID + DVE_POST
            DVE_ALL = GB * DVE_SEQ + DVE_GROUP

            def row_norm(src, par, vcount, before):
                dve.wait_ge(xn_ready, before)
                apart(dve)
                chain.step(nc.vector.bn_stats(bst[:, :], src))
                chain.settle()
                apart(dve)
                nc.vector.bn_aggr(mv[:, :], bst[:, :]).then_inc(var_ready, 1)
                dve.wait_ge(rstd_ready, vcount)
                nc.vector.tensor_scalar(xn[:, par, :], src, mv[:, 0:1], rstd[:, :],
                                        ALU.subtract, ALU.mult).then_inc(xn_ready, 1)

            dve.wait_ge(params_in, 16 * PARAMS)
            with dve.Fori(0, NG) as g:
                with dve.Fori(0, GB) as b:
                    n = g * GB + b
                    hb = hb_seq(g, b)
                    chain.start(g * DVE_ALL + b * DVE_SEQ)
                    dve.wait_ge(x_in, n * 16 + 16)
                    row_norm(x_t[:, :], 0, g * (LN_GROUP + 1) + b * 2 + 1, g * LN_GROUP + b * 2 + 2)
                    ready(dve, hb, TQ)
                    nc.vector.tensor_tensor(qT[:, :, :], dense[TQ % 2][:, 0:T].rearrange("p (e t) -> p e t", e=E),
                                            colb("q_b", LQ), ALU.add).then_inc(dense_free[TQ % 2], 1)
                    dve.wait_ge(maskb_ready, n + 1)

                    def normalise(k):
                        dve.wait_ge(pv_ready, n * H + 8 * (k + 1))
                        o = obank[k][0:LQ, 0:8 * (HD + 1)].rearrange("p (h d) -> p h d", h=8)
                        chain.step(nc.vector.reciprocal(rden[:, 8 * k:8 * k + 8], o[:, :, HD]))
                        chain.settle()
                        nc.vector.tensor_tensor(on[:, 256 * k:256 * (k + 1)].rearrange("p (h d) -> p h d", h=8),
                                                o[:, :, 0:HD],
                                                rden[:, 8 * k:8 * k + 8].unsqueeze(2).to_broadcast([LQ, 8, HD]),
                                                ALU.mult).then_inc(on_ready, 1)

                    for u in range(H):
                        dve.wait_ge(score_ready, n * H + (u + 1))
                        if u >= 2:
                            dve.wait_ge(prob_ready, n * H + (u - 1))
                        apart(dve)
                        nc.vector.tensor_tensor_reduce(
                            out=sm[:, u % 2, :], in0=score[u % 2][0:LQ, 0:LK], in1=maskb[:, :], scale=-SCALE,
                            scalar=3.0e38, op0=ALU.add, op1=ALU.min,
                            accum_out=nm[:, u % 2:u % 2 + 1]).then_inc(sm_ready, 1)
                        if u == 11:
                            normalise(0)
                    normalise(1)
                    ready(dve, hb, TO)
                    nc.vector.tensor_tensor(onT[:, :, :], dense[TO % 2][:, 0:T].rearrange("p (e t) -> p e t", e=E),
                                            colb("v_b", LQ), ALU.add).then_inc(dense_free[TO % 2], 1)
                    ready(dve, hb, TC)
                    dve.wait_ge(res_ready, n + 1)
                    dve.wait_ge(out_done, g * 64 + 16)
                    nc.vector.tensor_tensor(X[:, b, :], dense[TC % 2][0:LQ, :], res[:, :],
                                            ALU.add).then_inc(dense_free[TC % 2], 1)
                    evacuated(dve, hb, TC)
                    row_norm(X[:, b, :], 1, g * (LN_GROUP + 1) + b * 2 + 2, g * LN_GROUP + b * 2 + 3)
                    chain.end(DVE_SEQ)

                hb = hb_group(g)
                chain.start(g * DVE_ALL + GB * DVE_SEQ)
                dve.wait_ge(xn_ready, g * LN_GROUP + 10)
                chain.step(nc.vector.tensor_tensor(X[:, :, :], X[:, :, :],
                                                   pb[:, :].unsqueeze(1).to_broadcast([LQ, GB, D]), ALU.add))
                acc = [score[0], score[1], pT[0], pT[1]]
                for b in range(GB):
                    chain.settle()
                    dve.wait_ge(acc_ready, g * GB + (b + 1))
                    chain.step(nc.vector.tensor_tensor(X[:, b, :], X[:, b, :], acc[b][0:LQ, :], ALU.add))
                    chain.settle()
                    if b >= 2:
                        ready(dve, hb, G_LN1 + b - 2)
                    row_norm(X[:, b, :], b % 2, g * (LN_GROUP + 1) + (9 + b), g * LN_GROUP + (10 + b))

                def shift(which):
                    chain.step(nc.vector.tensor_copy(XA[:, :, :, 0], shc[:, which, :, bass.ds(g * GB, GB)]))
                    chain.settle()
                    chain.step(nc.vector.tensor_tensor(SX[:, :, :], XAc[:, :, 0:LQ], XAc[:, :, 1:LQ + 1],
                                                       ALU.subtract))
                    chain.settle()

                def mix_with(dst, name):
                    for e in range(E):
                        last = nc.vector.scalar_tensor_tensor(
                            out=dst[:, e, :].rearrange("p (b t) -> p b t", b=GB), in0=SX[:, GB * e:GB * (e + 1), :],
                            scalar=col(name, e), in1=XAs[:, e, :, :], op0=ALU.mult, op1=ALU.add)
                    return last

                evacuated(dve, hb, G_LN1 + 2)
                evacuated(dve, hb, G_LN1 + 3)
                shift(1)
                mix_with(C[0], "maa_x").then_inc(mix_ready, 1)
                for j in range(5):
                    dst = C[j % 2]
                    if j == 0:
                        ready(dve, hb, G_W1)
                    for e in range(E):
                        k = X_AT[j] + e
                        ready(dve, hb, k)
                        nc.vector.scalar_tensor_tensor(
                            out=dst[:, e, :], in0=dense[k % 2][:, 0:T], scalar=col(f"maa_{ORDER[j]}", e),
                            in1=SX[:, GB * e:GB * (e + 1), :].rearrange("p b t -> p (b t)"),
                            op0=ALU.add, op1=ALU.mult).then_inc(dense_free[k % 2], 1)
                    for e in range(E):
                        evacuated(dve, hb, X_AT[j] + e)
                        ins = nc.vector.tensor_tensor(dst[:, e, :].rearrange("p (b t) -> p b t", b=GB),
                                                      dst[:, e, :].rearrange("p (b t) -> p b t", b=GB),
                                                      XAs[:, e, :, :], ALU.add)
                        if e == E - 1:
                            ins.then_inc(mix_ready, 1)
                chain.step(nc.vector.memset(YB[:, :, :], 0.0))
                chain.step(nc.vector.memset(bon[:, 0, :], 0.0))
                chain.end(DVE_PRE)

                dve.wait_ge(v_in, g * 80 + 80)
                apart(dve)
                base = g * DVE_ALL + (GB * DVE_SEQ + DVE_PRE)

                def channel(i, par):
                    r, kk = rkw[:, par, 0, :], rkw[:, par, 1, :]
                    chain.step(nc.vector.scalar_tensor_tensor(out=bon[:, 1, :], in0=r,
                                                              scalar=ucol[:, bass.ds(i, 1)],
                                                              in1=kk, op0=ALU.mult, op1=ALU.mult))
                    for jh in range(RS // JH):
                        js = slice(jh * JH, (jh + 1) * JH)
                        chain.settle()
                        chain.step(nc.vector.tensor_tensor(S[:, :, 1:LQ], VB[:, js, 0:LQ - 1],
                                                           kk[:, 0:LQ - 1].unsqueeze(1).to_broadcast([P, JH, LQ - 1]),
                                                           ALU.mult))
                        s0i = s0[:, bass.ds(i, 1), js].rearrange("p a j -> p (a j)")
                        chain.step(nc.vector.tensor_copy(S[:, :, 0], s0i))
                        if jh == 0:
                            chain.step(nc.vector.tensor_tensor(bon[:, 0, :], bon[:, 0, :], bon[:, 1, :], ALU.add))
                            dve.wait_ge(wrep_ready, g * RS + (i + 1))
                        chain.settle()
                        chain.step(nc.vector.tensor_tensor_scan(
                            out=S[:, :, :].rearrange("p j t -> p (j t)"),
                            data0=wrep[:, par, :, :].rearrange("p j t -> p (j t)"),
                            data1=S[:, :, :].rearrange("p j t -> p (j t)"), initial=0.0, op0=ALU.mult, op1=ALU.add))
                        chain.settle()
                        rb = r.unsqueeze(1).to_broadcast([P, JH, LQ])
                        chain.step(nc.vector.tensor_tensor(S[:, :, :], S[:, :, :], rb, ALU.mult))
                        chain.settle()
                        ins = nc.vector.tensor_tensor(YB[:, js, :], YB[:, js, :], S[:, :, :], ALU.add)
                        if jh == RS // JH - 1:
                            ins.then_inc(scan_step, 1)
                        else:
                            chain.step(ins)

                with dve.Fori(0, RS // 2) as ip:
                    chain.start(base + ip * DVE_PAIR)
                    for par in range(2):
                        dve.wait_ge(rkw_in[par], g * 128 + ip * 16 + 16)
                        channel(ip * 2 + par, par)
                        dve.wait_ge(scan_step, g * RS + (ip * 2 + par + 1))
                        apart(dve)
                    chain.end(DVE_PAIR)

                chain.start(base + DVE_PAIR * (RS // 2))

                def over_j(v):
                    return v.unsqueeze(1).to_broadcast([P, RS, LQ])

                chain.step(nc.vector.tensor_tensor(VB[:, :, :], VB[:, :, :], over_j(bon[:, 0, :]), ALU.mult))
                chain.settle()
                chain.step(nc.vector.tensor_tensor(YB[:, :, :], YB[:, :, :], VB[:, :, :], ALU.add))
                chain.settle()
                chain.step(nc.vector.tensor_reduce(gst[:, 0, :], YB[:, :, :].rearrange("p j t -> p t j"),
                                                   axis=AX.X, op=ALU.add))
                chain.settle()
                chain.step(nc.vector.tensor_scalar(gst[:, 0, :], gst[:, 0, :], 1.0 / RS, None, ALU.mult))
                chain.settle()
                chain.step(nc.vector.tensor_tensor(YB[:, :, :], YB[:, :, :], over_j(gst[:, 0, :]), ALU.subtract))
                chain.settle()
                chain.step(nc.vector.tensor_tensor(VB[:, :, :], YB[:, :, :], YB[:, :, :], ALU.mult))
                chain.settle()
                nc.vector.tensor_reduce(gst[:, 1, :], VB[:, :, :].rearrange("p j t -> p t j"),
                                        axis=AX.X, op=ALU.add).then_inc(var_ready, 1)
                dve.wait_ge(rstd_ready, g * (LN_GROUP + 1) + 13)
                nc.vector.tensor_tensor(YB[:, :, :], YB[:, :, :], over_j(gst[:, 2, :]), ALU.mult).then_inc(y_norm, 1)
                chain.end(DVE_MID)

                chain.start(base + (DVE_PAIR * (RS // 2) + DVE_MID))
                dve.wait_ge(y_in, g * 64 + 64)
                for e in range(E):
                    ins = nc.vector.tensor_scalar(C[0][:, e, :], C[0][:, e, :], col("gn_w", e), col("gn_b", e),
                                                  ALU.mult, ALU.add)
                chain.step(ins)
                chain.settle()
                evacuated(dve, hb, P_AT[4] + 2)
                evacuated(dve, hb, P_AT[4] + 3)
                nc.vector.tensor_tensor(C[0][:, :, :], C[0][:, :, :], GT[:, :, :], ALU.mult).then_inc(mix_ready, 1)
                for b in range(GB):
                    k = G_OUT + b
                    ready(dve, hb, k)
                    nc.vector.tensor_tensor(X[:, b, :], X[:, b, :], dense[k % 2][0:LQ, :],
                                            ALU.add).then_inc(dense_free[k % 2], 1)
                    evacuated(dve, hb, k)
                    if b >= 2:
                        ready(dve, hb, G_LN2 + b - 2)
                    row_norm(X[:, b, :], b % 2, g * (LN_GROUP + 1) + (14 + b), g * LN_GROUP + (14 + b))
                evacuated(dve, hb, G_LN2 + 2)
                evacuated(dve, hb, G_LN2 + 3)
                shift(0)
                chain.step(mix_with(C[0], "mix_k"))
                mix_with(C[1], "mix_r").then_inc(mix_ready, 1)
                for b in range(GB):
                    k = G_FRV + 2 * b + 1
                    evacuated(dve, hb, k - 1)
                    ready(dve, hb, k)
                    if b >= 2:
                        dve.wait_ge(out_ready, g * GB + (b - 1))
                    nc.vector.tensor_tensor(xn[:, b % 2, :], dense[k % 2][0:LQ, :], RR[b % 2],
                                            ALU.mult).then_inc(dense_free[k % 2], 1)
                    evacuated(dve, hb, k)
                    nc.vector.tensor_tensor(X[:, b, :], X[:, b, :], xn[:, b % 2, :], ALU.add).then_inc(out_ready, 1)
                dve.wait_ge(out_ready, g * GB + GB)
                apart(dve)
                chain.end(DVE_POST)

        @block.tensor
        def _(pe):
            pe.sem_inc(dense_ready, READY0)
            for k in range(SLOTS):
                pe.sem_inc(ring_used[k], 1)
            pe.wait_ge(consts_made, 1)
            pe.wait_ge(params_in, 16 * PARAMS)

            def product(out_ap, pairs):
                for k, (lhsT, rhs) in enumerate(pairs):
                    last = nc.tensor.matmul(out_ap, lhsT, rhs, start=(k == 0), stop=(k == len(pairs) - 1))
                return last

            def rows_to_cols(k, rows):
                for e in range(E):
                    last = nc.tensor.transpose(dense[k % 2][:, e * LQ:(e + 1) * LQ], rows[:, e * P:(e + 1) * P],
                                               ident[0:LQ, 0:LQ])
                last.then_inc(dense_ready, 1)

            with pe.Fori(0, NG) as g:
                with pe.Fori(0, GB) as b:
                    n = g * GB + b
                    hb = hb_seq(g, b)
                    pe.wait_ge(ctx_in, n * 16 + 16)
                    for e in range(E):
                        bank_free(pe, hb, TK + e)
                        product(dense[(TK + e) % 2][:, 0:LK],
                                [(Wk[:, c, e * P:(e + 1) * P], ctx_t[:, c, :]) for c in range(E)]
                                ).then_inc(dense_ready, 1)
                    for k in range(KC):
                        bank_free(pe, hb, TV + k)
                        product(dense[(TV + k) % 2][0:KW, :],
                                [(ctx_t[:, c, k * KW:(k + 1) * KW], Wv[:, c, :]) for c in range(E)]
                                ).then_inc(dense_ready, 1)
                    pe.wait_ge(xn_ready, g * LN_GROUP + b * 2 + (2 + 1))
                    bank_free(pe, hb, TX)
                    rows_to_cols(TX, xn[:, 0, :])
                    evacuated(pe, hb, TX)
                    bank_free(pe, hb, TQ)
                    for e in range(E):
                        last = product(dense[TQ % 2][:, e * LQ:(e + 1) * LQ],
                                       [(Wq[:, c, e * P:(e + 1) * P], xnT[:, c, :]) for c in range(E)])
                    last.then_inc(dense_ready, 1)

                    def scores(u):
                        if u >= 2:
                            pe.wait_ge(sm_ready, n * H + (u - 1))
                        r = HD * (u % 4)
                        nc.tensor.matmul(score[u % 2][0:LQ, 0:LK], qT[r:r + HD, u // 4, :], KT[r:r + HD, u // 4, :],
                                         start=True, stop=True).then_inc(score_ready, 1)

                    def turn(u):
                        pe.wait_ge(prob_ready, n * H + (u + 1))
                        if u >= 2:
                            pe.wait_ge(probT_ready, n * H + (u - 1))
                        for k in range(KC):
                            last = nc.tensor.transpose(pT[u % 2][0:KW, k * LQ:(k + 1) * LQ],
                                                       prob[:, u % 2, k * KW:(k + 1) * KW], ident[0:LQ, 0:LQ])
                        last.then_inc(pT_ready, 1)

                    def weigh(u):
                        pe.wait_ge(probT_ready, n * H + (u + 1))
                        at = (u % 8) * (HD + 1)
                        product(obank[u // 8][0:LQ, at:at + HD + 1],
                                [(probT[:, u % 2, k * LQ:(k + 1) * LQ], V[:, k, u, :]) for k in range(KC)]
                                ).then_inc(pv_ready, 1)

                    evacuated(pe, hb, TQ)
                    scores(0)
                    scores(1)
                    for u in range(H):
                        turn(u)
                        if u + 2 < H:
                            scores(u + 2)
                        if u >= 1:
                            weigh(u - 1)
                    weigh(H - 1)
                    pe.wait_ge(on_ready, n * 2 + 2)
                    bank_free(pe, hb, TO)
                    rows_to_cols(TO, on)
                    evacuated(pe, hb, TO)
                    bank_free(pe, hb, TC)
                    product(dense[TC % 2][0:LQ, :], [(onT[:, c, :], Wc[:, c, :]) for c in range(E)]
                            ).then_inc(dense_ready, 1)
                    pe.wait_ge(xn_ready, g * LN_GROUP + b * 2 + (2 + 2))
                    bank_free(pe, hb, TY)
                    rows_to_cols(TY, xn[:, 1, :])

                hb = hb_group(g)

                def piece(k):
                    pe.wait_ge(ring_in[k % SLOTS], g * 64 + 16 * (k // SLOTS + 1))
                    return ring[:, k % SLOTS, :, :]

                def channels_out(first, w, src, used=None):
                    for e in range(E):
                        bank_free(pe, hb, first + e)
                        product(dense[(first + e) % 2][:, 0:T],
                                [(w[:, c, e * P:(e + 1) * P], src[:, c, :]) for c in range(E)]
                                ).then_inc(dense_ready, 1)

                def release(k):
                    pe.wait_ge(dense_ready, 2 * hb + (READY0 + USED[k] + 1))
                    pe.sem_inc(ring_used[k % SLOTS], 1)

                acc = [score[0], score[1], pT[0], pT[1]]
                bank_free(pe, hb, G_FC + 1)
                for m in range(4):
                    w = piece(2 * m)
                    channels_out(G_FC + 4 * m, w, YT)
                    w = piece(2 * m + 1)
                    evacuated(pe, hb, G_FC + 4 * m + 2)
                    evacuated(pe, hb, G_FC + 4 * m + 3)
                    for b in range(GB):
                        for c in range(E):
                            last = nc.tensor.matmul(acc[b][0:LQ, :], HT[:, c, b * LQ:(b + 1) * LQ], w[:, c, :],
                                                    start=(m == 0 and c == 0), stop=(m == 3 and c == E - 1))
                        if m == 3:
                            last.then_inc(acc_ready, 1)
                    if m < 3:
                        last.then_inc(mlp_used, 1)
                        pe.wait_ge(mlp_used, g * 4 + (m + 1))
                    else:
                        pe.wait_ge(acc_ready, g * GB + GB)
                    if m == 3:
                        pe.sem_inc(mlp_used, 1)
                    pe.sem_inc(ring_used[(2 * m) % SLOTS], 1)
                    pe.sem_inc(ring_used[(2 * m + 1) % SLOTS], 1)

                for b in range(GB):
                    pe.wait_ge(xn_ready, g * LN_GROUP + (2 + 9 + b))
                    bank_free(pe, hb, G_LN1 + b)
                    rows_to_cols(G_LN1 + b, xn[:, b % 2, :])
                pe.wait_ge(mix_ready, g * 8 + 1)
                bank_free(pe, hb, G_W1)
                product(dense[G_W1 % 2][:, 0:T], [(mw1[:, c, 0:P], C[0][:, c, :]) for c in range(E)])
                product(score[0][0:DM, 0:T], [(mw1[:, c, P:5 * DM], C[0][:, c, :]) for c in range(E)]
                        ).then_inc(dense_ready, 1)

                def low_rank(j):
                    q = ORDER[j]
                    w, a = (mw2b, TB) if q == 4 else (mw2[DM * q:DM * (q + 1), :], TA[DM * q:DM * (q + 1), :])
                    for e in range(E):
                        k = X_AT[j] + e
                        bank_free(pe, hb, k)
                        nc.tensor.matmul(dense[k % 2][:, 0:T], w[:, e * P:(e + 1) * P], a[:, :] if q == 4 else a,
                                         start=True, stop=True).then_inc(dense_ready, 1)

                evacuated(pe, hb, G_W1)
                low_rank(0)
                low_rank(1)
                pe.wait_ge(mix_ready, g * 8 + 2)
                bank_free(pe, hb, TD1)
                product(dense[TD1 % 2][0:DD, 0:T], [(tw1[:, c, :], C[0][:, c, :]) for c in range(E)]
                        ).then_inc(dense_ready, 1)
                evacuated(pe, hb, TD1)
                for e in range(E):
                    k = TD2 + e
                    bank_free(pe, hb, k)
                    nc.tensor.matmul(dense[k % 2][:, 0:T], tw2[:, e * P:(e + 1) * P], TD,
                                     start=True, stop=True).then_inc(dense_ready, 1)
                for j in range(2, 6):
                    if j < 5:
                        low_rank(j)
                    w = piece(8 + j - 2)
                    pe.wait_ge(mix_ready, g * 8 + (j + 1))
                    channels_out(P_AT[j - 1], w, C[(j - 1) % 2])
                    pe.wait_ge(dense_ready, 2 * hb + (READY0 + P_AT[j - 1] + 4))
                    pe.sem_inc(ring_used[(8 + j - 2) % SLOTS], 1)

                w = piece(12)
                pe.wait_ge(mix_ready, g * 8 + 7)
                for b in range(GB):
                    k = G_OUT + b
                    bank_free(pe, hb, k)
                    product(dense[k % 2][0:LQ, :], [(C[0][:, c, b * LQ:(b + 1) * LQ], w[:, c, :]) for c in range(E)]
                            ).then_inc(dense_ready, 1)
                pe.wait_ge(dense_ready, 2 * hb + (READY0 + G_OUT + 4))
                pe.sem_inc(ring_used[12 % SLOTS], 1)
                for b in range(GB):
                    pe.wait_ge(xn_ready, g * LN_GROUP + (2 + 13 + b))
                    bank_free(pe, hb, G_LN2 + b)
                    rows_to_cols(G_LN2 + b, xn[:, b % 2, :])
                w = piece(13)
                pe.wait_ge(mix_ready, g * 8 + 8)
                channels_out(G_FK, w, C[0])
                wr = piece(14)
                wv_ = piece(15)
                for b in range(GB):
                    k = G_FRV + 2 * b
                    bank_free(pe, hb, k)
                    product(dense[k % 2][0:LQ, :], [(C[1][:, c, b * LQ:(b + 1) * LQ], wr[:, c, :]) for c in range(E)]
                            ).then_inc(dense_ready, 1)
                    if b == 0:
                        pe.wait_ge(kk_ready, g * E + E)
                    bank_free(pe, hb, k + 1)
                    product(dense[(k + 1) % 2][0:LQ, :],
                            [(HT[:, c, b * LQ:(b + 1) * LQ], wv_[:, c, :]) for c in range(E)]
                            ).then_inc(dense_ready, 1)
                pe.wait_ge(dense_ready, 2 * hb + (READY0 + G_FRV + 8))
                for k in (13, 14, 15):
                    pe.sem_inc(ring_used[k % SLOTS], 1)


def kernel(x, ctx_2048, mask_BxS2_bf1, **p):
    import concourse.bacc as bacc
    from concourse.bass_utils import run_bass_kernel_spmd

    a = {k: np.asarray(v) for k, v in p.items()}
    x, ctx, mask = np.asarray(x), np.asarray(ctx_2048), np.asarray(mask_BxS2_bf1)
    l0 = {k[len("L0_xattn_"):]: v for k, v in a.items() if k.startswith("L0_xattn_")}
    l1 = {k[len("L1_xattn_"):]: v for k, v in a.items() if k.startswith("L1_xattn_")}
    vecs = [l0["ln1_w"], l0["ln1_b"], l0["q_b"], l0["k_b"], l0["v_b"], l0["ln2_w"], l0["ln2_b"],
            l1["ln1_w"], l1["ln1_b"], l1["ln2_w"], l1["ln2_b"], l1["maa_x"],
            *[l1["maa_stack"][0, j] for j in range(5)], l1["time_decay"], l1["gn_w"], l1["gn_b"],
            l1["ffn_maa_k"], l1["ffn_maa_r"], l0["fc_b"]]
    cols = np.concatenate([v.reshape(-1, P).T for v in vecs], axis=1)
    pieces = []
    for m in range(4):
        pieces += [l0["fc_w"][:, m * D:(m + 1) * D], l0["proj_w"][m * D:(m + 1) * D, :]]
    pieces += [l1[w].T for w in ("Wk", "Wv", "Wr", "Wg", "Wo", "Wfk", "Wfr", "Wfv")]
    arrays = {
        "x": x,
        "ctxT": ctx.transpose(0, 2, 1),
        "ctx": ctx,
        "mask": mask.view(np.uint8),
        "shiftcols": ctx[:, 0:2, :].reshape(B, 2, E, P).transpose(3, 1, 2, 0),
        "cols": cols,
        "wq": l0["q_w"], "wk": l0["k_w"], "wv": l0["v_w"], "wc": l0["cproj_w"],
        "cproj_b": l0["cproj_b"], "proj_b": l0["proj_b"],
        "stream": np.stack(pieces),
        "maa_w1": l1["maa_w1"], "maa_w2": l1["maa_w2"].reshape(5 * DM, D),
        "td_w1": l1["td_w1"], "td_w2": l1["td_w2"],
        "u": np.tile(l1["u"].reshape(RH, RS), (GB, 1)),
    }
    arrays = {f"in_{k}": np.ascontiguousarray(v) for k, v in arrays.items()}
    nc = bacc.Bacc("TRN2", target_bir_lowering=False, num_devices=1)
    args = [nc.dram_tensor(k, v.shape, mybir.dt.from_np(v.dtype), kind="ExternalInput").ap()
            for k, v in arrays.items()]
    out = nc.dram_tensor("out", (B, LQ, D), F32, kind="ExternalOutput").ap()
    build(nc, *args, out)
    r = run_bass_kernel_spmd(nc, [arrays], core_ids=[0])
    return r.results[0]["out"]
```

```python
import numpy as np
import concourse.bass as bass
import concourse.mybir as mybir
from contextlib import ExitStack

F32 = mybir.dt.float32
U8 = mybir.dt.uint8
ALU = mybir.AluOpType
ACT = mybir.ActivationFunctionType
AX = mybir.AxisListType

B, LQ, LK, D = 16, 112, 375, 512
P = 128
E = D // P
H, HD = 16, 32
INNER = 4 * D
GB = 4
NG = B // GB
T = GB * LQ
KC = 3
KW = LK // KC
RH, RS = 32, 16
JH = 8
DM, DD = 32, 64
EPS = 1e-5
SCALE = float(np.float32(1.0) / np.sqrt(np.float32(HD)))
BIG = float(2.0 ** 126)
SLOTS = 2

COLS = ["ln1_w", "ln1_b", "q_b", "k_b", "v_b", "ln2_w", "ln2_b",
        "r_ln1_w", "r_ln1_b", "r_ln2_w", "r_ln2_b", "maa_x",
        "maa_0", "maa_1", "maa_2", "maa_3", "maa_4", "decay", "gn_w", "gn_b", "mix_k", "mix_r"]
FCB = E * len(COLS)
NCOL = FCB + INNER // P
ORDER = [1, 0, 2, 3, 4]

TK, TV0, TX, TQ, TV1, TO, TC, TV2, TY = 0, 4, 5, 6, 7, 8, 9, 10, 11
SEQ_TILES = 12
PK, PV0, PXA, PXB, PQ, PV1, PV2 = 0, 4, 5, 6, 7, 8, 9
FIRST_TILES = 10
MLP_TILES = 16
POST_TILES = 20
O_OUT, O_LN, O_FK, O_FRV = 0, 4, 8, 12
PRE_TILES = 46
R_LN, R_W1 = 0, 4
X_AT = [5, 9, 18, 26, 34]
TD1, TD2 = 13, 14
P_AT = [None, 22, 30, 38, 42]
READY0 = 1

STEP0 = GB * SEQ_TILES + MLP_TILES + PRE_TILES
STEP = STEP0 + POST_TILES
W_MLP, W_OUT, W_PROJ = range(0, 8), range(12, 16), range(8, 12)


def half_step(g):
    return FIRST_TILES // 2 if isinstance(g, int) and g == 0 else g * (STEP // 2) + (FIRST_TILES + STEP0 - STEP) // 2


def half_seq(g, b):
    return half_step(g) + b * (SEQ_TILES // 2)


def half_mlp(g):
    return half_step(g) + GB * SEQ_TILES // 2


def half_post(g):
    return half_step(g) if isinstance(g, int) and g == NG else half_mlp(g) + MLP_TILES // 2


def half_pre(g):
    first = isinstance(g, int) and g == 0
    return half_mlp(g) + (MLP_TILES + (0 if first else POST_TILES)) // 2


def pieces_of(g):
    first, last = isinstance(g, int) and g == 0, isinstance(g, int) and g == NG
    return [*([] if last else W_MLP), *([] if first else W_OUT), *([] if last else W_PROJ)]


def half_piece(g):
    return 0 if isinstance(g, int) and g == 0 else g * 8 - 2


class Chain:

    def __init__(self, engine, sem):
        self.engine, self.sem, self.base, self.count = engine, sem, 0, 0

    def start(self, base):
        self.base, self.count = base, 0

    def step(self, instruction):
        self.count += 1
        instruction.then_inc(self.sem, 1)

    def settle(self):
        self.engine.wait_ge(self.sem, self.base + self.count)

    def end(self, count):
        assert self.count == count, (self.count, count)


def build(nc, x, ctxT, ctx, mask, shiftcols, cols, wq, wk, wv, wc, cproj_b, proj_b, stream,
          maa_w1, maa_w2, td_w1, td_w2, u, out):
    rkw_d = nc.dram_tensor("rkw_scratch", (B * RH, RS, 3, LQ), F32, kind="Internal").ap()
    v_d = nc.dram_tensor("v_scratch", (B * RH, RS * LQ), F32, kind="Internal").ap()
    y_d = nc.dram_tensor("y_scratch", (B * RH, RS * LQ), F32, kind="Internal").ap()

    ctxm = ExitStack()
    with ctxm:
        def sb(name, shape, dt=F32):
            return ctxm.enter_context(nc.sbuf_tensor(name, shape, dt))

        def sem(name):
            return ctxm.enter_context(nc.semaphore(name))

        ident = sb("ident", [P, P])
        colt = sb("colt", [P, NCOL])
        Wq, Wk, Wv, Wc = (sb(n, [P, E, D]) for n in ("Wq", "Wk", "Wv", "Wc"))
        ring = sb("ring", [P, SLOTS, E, D])
        mw1 = sb("mw1", [P, E, 5 * DM])
        mw2 = sb("mw2", [P, D])
        mw2b = sb("mw2b", [DM, D])
        tw1 = sb("tw1", [P, E, DD])
        tw2 = sb("tw2", [DD, D])
        cb = sb("cb", [LQ, D])
        pb = sb("pb", [LQ, D])
        shc = sb("shc", [P, 2, E, B])
        ucol = sb("ucol", [P, RS])
        half = sb("half", [P, LQ])
        ctx_t = sb("ctx_t", [P, E, LK])
        x_t = sb("x_t", [LQ, D])
        res = sb("res", [LQ, D])
        xn = sb("xn", [LQ, 2, D])
        xnT = sb("xnT", [P, E, LQ])
        qT = sb("qT", [P, 2, E, LQ])
        KT = sb("KT", [P, 2, E, LK])
        V = sb("V", [KW, 2, KC, H, HD + 1])
        mrow = sb("mrow", [LQ, LK], U8)
        maskb = sb("maskb", [LQ, LK])
        sm = sb("sm", [LQ, 2, LK])
        nm = sb("nm", [LQ, 2])
        prob = sb("prob", [LQ, 2, LK])
        probT = sb("probT", [KW, 2, KC * LQ])
        rden = sb("rden", [LQ, H])
        on = sb("on", [LQ, D])
        onT = sb("onT", [P, E, LQ])
        PH = ("seq", "pre", "post")
        bst = {p: sb(f"bst_{p}", [LQ, 6]) for p in PH}
        mv = {p: sb(f"mv_{p}", [LQ, 2]) for p in PH}
        vare = {p: sb(f"vare_{p}", [LQ, 1]) for p in PH}
        rstd = {p: sb(f"rstd_{p}", [LQ, 1]) for p in PH}
        X = sb("X", [LQ, 2 * GB, D])
        XA = sb("XA", [P, E, GB, LQ + 1])
        SX = sb("SX", [P, E * GB, LQ])
        C = [sb("C0", [P, E, T]), sb("C1", [P, E, T])]
        HT = sb("HT", [P, E, T])
        GT = sb("GT", [P, E, T])
        TA = sb("TA", [P, T])
        TB = sb("TB", [DM, T])
        VB = sb("VB", [P, RS, LQ])
        YB = sb("YB", [P, RS, LQ])
        rkw = sb("rkw", [P, 4, 3, LQ])
        s0 = sb("s0", [P, RS, RS])
        bon = sb("bon", [P, 2, LQ])
        gst = sb("gst", [P, 3, LQ])

        YT = SX[:, :, :].rearrange("p (e b) t -> p e (b t)", e=E)
        TD = GT[0:DD, 0, :]
        RR = [GT[0:LQ, :, :].rearrange("p e t -> p (e t)")[:, k * D:(k + 1) * D] for k in range(2)]
        XAs = XA[:, :, :, 1:LQ + 1]
        XAc = XA[:, :, :, :].rearrange("p e b t -> p (e b) t")
        S = C[1][:, :, :].rearrange("p e (b t) -> p (e b) t", b=GB)
        wrep = XA[:, :, :, :].rearrange("p e b t -> p (e b t)")[:, 0:2 * JH * LQ].rearrange(
            "p (s n) -> p s n", s=2)

        bank = [ctxm.enter_context(nc.psum_tensor(f"bank{k}", [P, 512], F32)) for k in range(8)]
        dense = bank[0:2]
        score = bank[2:4]
        pT = bank[4:6]
        obank = bank[6:8]
        acc = [score[0], score[1], pT[0], pT[1]]

        def col(name, e):
            k = COLS.index(name) * E + e
            return colt[:, k:k + 1]

        def colb(name, n):
            k = COLS.index(name) * E
            return colt[:, k:k + E].unsqueeze(2).to_broadcast([P, E, n])

        wk_in, wv_in, wq_in, cols_in = sem("wk_in"), sem("wv_in"), sem("wq_in"), sem("cols_in")
        params_in = sem("params_in")
        consts_made = sem("consts_made")
        ring_in = [sem(f"ring_in{k}") for k in range(SLOTS)]
        ring_used = [sem(f"ring_used{k}") for k in range(SLOTS)]
        x_in, ctx_in, mask_in = sem("x_in"), sem("ctx_in"), sem("mask_in")
        res_ready = sem("res_ready")
        maskb_ready = sem("maskb_ready")
        stats_ready = {p: sem(f"stats_ready_{p}") for p in PH}
        var_ready = {p: sem(f"var_ready_{p}") for p in (*PH, "gn")}
        rstd_ready = {p: sem(f"rstd_ready_{p}") for p in (*PH, "gn")}
        eps_added = {p: sem(f"eps_added_{p}") for p in (*PH, "gn")}
        xn_ready = {p: sem(f"xn_ready_{p}") for p in PH}
        dense_ready = sem("dense_ready")
        dense_free = [sem("dense_free0"), sem("dense_free1")]
        score_ready = sem("score_ready")
        sm_ready = sem("sm_ready")
        prob_ready = sem("prob_ready")
        pT_ready = sem("pT_ready")
        probT_ready = sem("probT_ready")
        pv_ready = sem("pv_ready")
        den_ready = sem("den_ready")
        on_ready = sem("on_ready")
        mlp_used = sem("mlp_used")
        acc_ready = sem("acc_ready")
        bias_added = sem("bias_added")
        x1_ready = sem("x1_ready")
        mix_ready = sem("mix_ready")
        shift_ready = {p: sem(f"shift_ready_{p}") for p in ("pre", "post")}
        gn_scaled = sem("gn_scaled")
        og_ready = sem("og_ready")
        ck_ready = sem("ck_ready")
        decay_ready = sem("decay_ready")
        e_out = [sem(f"e_out{k}") for k in range(E)]
        v_in = sem("v_in")
        rkw_in = sem("rkw_in")
        wrep_ready = sem("wrep_ready")
        scan_chain = sem("scan_chain")
        scan_step = sem("scan_step")
        gn_chain = sem("gn_chain")
        y_norm = sem("y_norm")
        y_out, y_in = sem("y_out"), sem("y_in")
        kk_ready = sem("kk_ready")
        out_ready = sem("out_ready")
        out_done = sem("out_done")
        carried = sem("carried")

        def apart(eng):
            eng.sem_inc(carried, 1)

        def ready(eng, hb, k):
            eng.wait_ge(dense_ready, 2 * hb + (READY0 + k + 1))

        def evacuated(eng, hb, k):
            eng.wait_ge(dense_free[k % 2], hb + (k // 2 + 2))

        def bank_free(eng, hb, k):
            eng.wait_ge(dense_free[k % 2], hb + (k // 2 + 1))

        PARAMS = 11
        CHANNEL = 7
        PAIRS = GB // 2

        def steps(eng, step):
            step(0)
            with eng.Fori(1, NG) as g:
                step(g)
            step(NG)

        def sequences(eng, g, seq):
            with eng.Fori(0, PAIRS) as bp:
                for par in range(2):
                    b = bp * 2 + par
                    seq(g, b, par, g * GB + b)

        block = ctxm.enter_context(nc.Block())

        def channels_loaded(gp, b):
            return gp * 160 + b * 32 + 32

        def load_channels(eng, gp, b):
            rows = rkw_d[bass.ds(gp * P, P), bass.ds(b * 4, 4), :, :]
            eng.dma_start(rkw[:, :, 0:2, :].rearrange("p q s t -> p q (s t)"),
                          rows[:, :, 0:2, :].rearrange("p q s t -> p q (s t)")).then_inc(rkw_in, 16)
            eng.dma_start(rkw[:, :, 2, 1:LQ], rows[:, :, 2, 0:LQ - 1]).then_inc(rkw_in, 16)

        @block.sync
        def _(sp):
            def load_ctx(n):
                sp.dma_start(ctx_t[:, :, :], ctxT[n % B, :, :].rearrange("(c p) t -> p c t", p=P)).then_inc(ctx_in, 16)

            def load_x(n):
                sp.dma_start(x_t[:, :], x[n % B, :, :]).then_inc(x_in, 16)

            def load_mask(n):
                sp.dma_start(mrow[:, :], mask[n % B, :].partition_broadcast(LQ)).then_inc(mask_in, 16)

            load_x(0)
            load_ctx(0)
            sp.dma_start(Wk[:, :, :], wk.rearrange("(c p) n -> p c n", p=P)).then_inc(wk_in, 16)
            sp.dma_start(Wv[:, :, :], wv.rearrange("(c p) n -> p c n", p=P)).then_inc(wv_in, 16)
            load_mask(0)
            sp.wait_ge(res_ready, 1)
            sp.wait_ge(xn_ready["seq"], 1)
            load_x(1)
            sp.wait_ge(maskb_ready, 1)
            load_mask(1)
            ready(sp, 0, PV2)
            load_ctx(1)

            def seq(g, b, par, n):
                ready(sp, half_seq(g, b), TV2)
                load_ctx(n + 2)
                sp.wait_ge(res_ready, n + 2)
                sp.wait_ge(xn_ready["seq"], n * 2 + 2)
                load_x(n + 2)
                sp.wait_ge(maskb_ready, n + 2)
                apart(sp)
                load_mask(n + 2)

            def step(g):
                first, last = isinstance(g, int) and g == 0, isinstance(g, int) and g == NG
                order = pieces_of(g)

                def piece(k):
                    sp.wait_ge(ring_used[k % SLOTS], half_piece(g) + (k // SLOTS + 1))
                    sp.dma_start(ring[:, k % SLOTS, :, :],
                                 stream[order[k]].rearrange("(c p) n -> p c n", p=P)).then_inc(ring_in[k % SLOTS], 16)

                if not first:
                    for e in range(E):
                        sp.wait_ge(e_out[e], g * 64)
                    sp.dma_start(VB[:, :, :].rearrange("p j t -> p (j t)"),
                                 v_d[bass.ds((g - 1) * P, P), :]).then_inc(v_in, 16)
                    for b in range(GB):
                        sp.dma_start(s0[RH * b:RH * (b + 1), :, :].rearrange("p i j -> p (i j)"),
                                     ctx[(g - 1) * GB + b, 2:2 + RS, :].rearrange("s (q c) -> (s q) c", c=RS * RS)
                                     ).then_inc(v_in, 16)
                piece(0)
                piece(1)
                if not last:
                    sequences(sp, g, seq)
                if not last:
                    piece(2)
                if not first:
                    sp.wait_ge(y_norm, g)
                    sp.dma_start(y_d[bass.ds((g - 1) * P, P), :],
                                 YB[:, :, :].rearrange("p j t -> p (j t)")).then_inc(y_out, 16)
                    sp.wait_ge(y_out, g * 16)
                    for b in range(GB):
                        sp.dma_start(C[0][:, :, b * LQ:(b + 1) * LQ],
                                     y_d[bass.ds((g - 1) * P + RH * b, RH), :].rearrange("h (j t) -> (h j) t", t=LQ)
                                     .rearrange("(e p) t -> p e t", p=P)).then_inc(y_in, 16)
                for k in range(2 if last else 3, len(order)):
                    piece(k)

            steps(sp, step)
            sp.wait_ge(out_done, 16 * B)
            sp.wait_ge(x_in, 16 * (B + 2))
            sp.wait_ge(ctx_in, 16 * (B + 2))
            sp.wait_ge(mask_in, 16 * (B + 2))

        @block.gpsimd
        def _(pool):
            nc.gpsimd.memset(ident[:, :], 0.0).then_inc(consts_made, 1)
            nc.gpsimd.memset(half[:, :], -0.5).then_inc(consts_made, 1)
            nc.gpsimd.memset(rkw[:, :, 2, 0:1], 0.0).then_inc(consts_made, 1)
            nc.gpsimd.memset(V[:, :, :, :, HD:HD + 1], 1.0).then_inc(consts_made, 1)
            pool.wait_ge(consts_made, 4)
            nc.gpsimd.affine_select(out=ident[:, :], in_=ident[:, :], compare_op=ALU.not_equal, fill=1.0,
                                    base=0, pattern=[[-1, P]], channel_multiplier=1).then_inc(consts_made, 1)

            def inv_std(p, count):
                pool.wait_ge(var_ready[p], count)
                apart(pool)
                if p == "gn":
                    src, tmp, dst, scale, n = gst[:, 1, :], gst[:, 2, :], gst[:, 2, :], 1.0 / RS, LQ
                    expo = half[:, :]
                else:
                    src, tmp, dst, scale = mv[p][:, 1:2], vare[p][:, :], rstd[p][:, :], 1.0
                    expo = half[0:LQ, 0:1]
                nc.gpsimd.tensor_scalar(tmp, src, scale, EPS, ALU.mult, ALU.add).then_inc(eps_added[p], 1)
                pool.wait_ge(eps_added[p], count)
                nc.gpsimd.tensor_tensor(dst, tmp, expo, ALU.pow).then_inc(rstd_ready[p], 1)

            def residual(n):
                pool.wait_ge(x_in, n * 16 + 16)
                nc.gpsimd.tensor_tensor(res[:, :], x_t[:, :], cb[:, :], ALU.add).then_inc(res_ready, 1)

            def mask_rows(n):
                pool.wait_ge(mask_in, n * 16 + 16)
                apart(pool)
                nc.gpsimd.tensor_scalar(maskb[:, :], mrow[:, :], BIG, -BIG, ALU.mult, ALU.add).then_inc(maskb_ready, 1)

            inv_std("seq", 1)
            pool.wait_ge(params_in, 16 * PARAMS)
            residual(0)
            mask_rows(0)

            def seq(scan):
                def body(g, b, par, n):
                    inv_std("seq", n * 2 + 2)
                    if scan:
                        pool.wait_ge(scan_step, (g - 1) * RS + b * 4 + 5)
                        load_channels(pool, g - 1, (b + 1) % GB)
                    inv_std("seq", n * 2 + 3)
                    evacuated(pool, half_seq(g, b), TC)
                    mask_rows(n + 1)
                    residual(n + 1)
                return body

            def step(g):
                first, last = isinstance(g, int) and g == 0, isinstance(g, int) and g == NG
                if not first:
                    for e in range(E):
                        pool.wait_ge(e_out[e], g * 64)
                    load_channels(pool, g - 1, 0)
                if not last:
                    sequences(pool, g, seq(not first))
                else:
                    for b in range(GB):
                        pool.wait_ge(scan_step, (g - 1) * RS + b * 4 + 5)
                        if b < GB - 1:
                            load_channels(pool, g - 1, b + 1)
                if not first:
                    pool.wait_ge(rkw_in, g * 160 if not last else g * 160 - 32)
                    inv_std("gn", g)
                    for b in range(GB):
                        inv_std("post", (g - 1) * GB + (b + 1))
                    for b in range(GB):
                        pool.wait_ge(out_ready, (g - 1) * GB + (b + 1))
                        pool.dma_start(out[(g - 1) * GB + b, :, :],
                                       X[:, ((g - 1) % 2) * GB + b, :]).then_inc(out_done, 16)
                if last:
                    return
                for b in range(GB):
                    inv_std("pre", g * GB + (b + 1))
                hb = half_pre(g)

                def store(which, e):
                    rows = bass.ds(g * P, P)
                    if which == 3:
                        dst = v_d[rows, :].rearrange("(b h) (j t) -> b (h j) t", b=GB, t=LQ)[:, e * P:(e + 1) * P, :]
                    else:
                        dst = rkw_d[rows, :, :, :].rearrange("(b h) i s t -> b (h i) s t", b=GB)[
                            :, e * P:(e + 1) * P, which, :]
                    pool.dma_start(dst.rearrange("b p t -> p b t"),
                                   HT[:, e, :].rearrange("p (b t) -> p b t", b=GB)).then_inc(e_out[e], 16)

                for e in range(E):
                    pool.wait_ge(decay_ready, g * E + (e + 1))
                    store(2, e)
                for j, which in ((1, 1), (2, 3), (3, 0)):
                    for e in range(E):
                        evacuated(pool, hb, P_AT[j] + e)
                        store(which, e)

            steps(pool, step)

        @block.scalar
        def _(act):
            act.sem_inc(dense_free[0], 1)
            act.sem_inc(dense_free[1], 1)
            act.dma_start(colt[:, :], cols).then_inc(cols_in, 16)
            act.dma_start(Wq[:, :, :], wq.rearrange("(c p) n -> p c n", p=P)).then_inc(wq_in, 16)
            act.dma_start(cb[:, :], cproj_b.partition_broadcast(LQ)).then_inc(params_in, 16)
            act.dma_start(Wc[:, :, :], wc.rearrange("(c p) n -> p c n", p=P)).then_inc(params_in, 16)
            act.dma_start(pb[:, :], proj_b.partition_broadcast(LQ)).then_inc(params_in, 16)
            act.dma_start(mw1[:, :, :], maa_w1.rearrange("(c p) n -> p c n", p=P)).then_inc(params_in, 16)
            act.dma_start(mw2[:, :], maa_w2[0:P, :]).then_inc(params_in, 16)
            act.dma_start(mw2b[:, :], maa_w2[P:5 * DM, :]).then_inc(params_in, 16)
            act.dma_start(tw1[:, :, :], td_w1.rearrange("(c p) n -> p c n", p=P)).then_inc(params_in, 16)
            act.dma_start(tw2[:, :], td_w2).then_inc(params_in, 16)
            act.dma_start(shc[:, 0, :, :], shiftcols[:, 0, :, :]).then_inc(params_in, 16)
            act.dma_start(shc[:, 1, :, :], shiftcols[:, 1, :, :]).then_inc(params_in, 16)
            act.dma_start(ucol[:, :], u).then_inc(params_in, 16)
            act.wait_ge(cols_in, 16)

            def copy_cols(dst, psum, w, bcol, e):
                return nc.scalar.activation(dst, psum, ACT.Identity, bias=col(bcol, e), scale=col(w, e))

            def keys(hb, k, e, half_):
                ready(act, hb, k)
                nc.scalar.activation(KT[:, half_, e, :], dense[k % 2][:, 0:LK], ACT.Identity,
                                     bias=col("k_b", e)).then_inc(dense_free[k % 2], 1)

            def values(hb, k, chunk, half_):
                ready(act, hb, k)
                nc.scalar.activation(V[:, half_, chunk, :, 0:HD],
                                     dense[k % 2][0:KW, :].rearrange("p (h d) -> p h d", h=H),
                                     ACT.Copy).then_inc(dense_free[k % 2], 1)

            for e in range(E):
                keys(0, PK + e, e, 0)
            act.wait_ge(consts_made, 5)
            values(0, PV0, 0, 0)
            for k, es in ((PXA, (0, 1)), (PXB, (2, 3))):
                ready(act, 0, k)
                for e in es:
                    last_ = copy_cols(xnT[:, e, :], dense[k % 2][:, (e % 2) * LQ:(e % 2 + 1) * LQ], "ln1_w", "ln1_b", e)
                last_.then_inc(dense_free[k % 2], 1)
            values(0, PV1, 1, 0)
            values(0, PV2, 2, 0)

            def repeat_decays(gp, b, q):
                act.wait_ge(rkw_in, channels_loaded(gp, b))
                if q >= 2:
                    act.wait_ge(scan_step, gp * RS + b * 4 + q)
                nc.scalar.activation(wrep[:, q % 2, :].rearrange("p (j t) -> p j t", j=JH),
                                     rkw[:, q, 2, :].unsqueeze(1).to_broadcast([P, JH, LQ]),
                                     ACT.Copy).then_inc(wrep_ready, 1)

            def seq(scan):
                def body(g, b, par, n):
                    hb, nxt = half_seq(g, b), 1 - par

                    def move_pT(u):
                        act.wait_ge(pT_ready, n * H + (u + 1))
                        if u >= 2:
                            act.wait_ge(pv_ready, n * H + (u - 1))
                        nc.scalar.activation(probT[:, u % 2, :], pT[u % 2][0:KW, 0:KC * LQ],
                                             ACT.Copy).then_inc(probT_ready, 1)

                    for u in range(H):
                        act.wait_ge(sm_ready, n * H + (u + 1))
                        if u >= 2:
                            act.wait_ge(pT_ready, n * H + (u - 1))
                        nc.scalar.activation(prob[:, u % 2, :], sm[:, u % 2, :], ACT.Exp,
                                             bias=nm[:, u % 2:u % 2 + 1], scale=-1.0).then_inc(prob_ready, 1)
                        if u >= 1:
                            move_pT(u - 1)
                        if scan and u in (0, 3, 7, 11):
                            repeat_decays(g - 1, b, (u + 1) // 4)
                        if u in (1, 3, 5, 7):
                            keys(hb, TK + u // 2, u // 2, nxt)
                        elif u == 9:
                            values(hb, TV0, 0, nxt)
                        elif u == 10:
                            ready(act, hb, TX)
                            for e in range(E):
                                last_ = copy_cols(xnT[:, e, :], dense[TX % 2][:, e * LQ:(e + 1) * LQ],
                                                  "ln1_w", "ln1_b", e)
                            last_.then_inc(dense_free[TX % 2], 1)
                    move_pT(H - 1)
                    values(hb, TV1, 1, nxt)
                    values(hb, TV2, 2, nxt)
                    ready(act, hb, TY)
                    for e in range(E):
                        last_ = copy_cols(YT[:, e, bass.ds(b * LQ, LQ)], dense[TY % 2][:, e * LQ:(e + 1) * LQ],
                                          "ln2_w", "ln2_b", e)
                    last_.then_inc(dense_free[TY % 2], 1)
                return body

            def ln_cols(hb, first_tile, w, bcol):
                for b in range(GB):
                    k = first_tile + b
                    ready(act, hb, k)
                    for e in range(E):
                        last_ = copy_cols(XA[:, e, b, 1:LQ + 1], dense[k % 2][:, e * LQ:(e + 1) * LQ], w, bcol, e)
                    last_.then_inc(dense_free[k % 2], 1)

            def mlp(g):
                hb = half_mlp(g)
                for m in range(4):
                    if m >= 1:
                        act.wait_ge(mlp_used, g * 3 + m)
                    for e in range(E):
                        k = 4 * m + e
                        ready(act, hb, k)
                        nc.scalar.activation(HT[:, e, :], dense[k % 2][:, 0:T], ACT.Gelu_apprx_tanh,
                                             bias=colt[:, FCB + k:FCB + k + 1]).then_inc(dense_free[k % 2], 1)

            def post(g):
                hb = half_post(g)
                ln_cols(hb, O_LN, "r_ln2_w", "r_ln2_b")
                for e in range(E):
                    k = O_FK + e
                    ready(act, hb, k)
                    nc.scalar.activation(HT[:, e, :], dense[k % 2][:, 0:T], ACT.Relu).then_inc(dense_free[k % 2], 1)
                for e in range(E):
                    evacuated(act, hb, O_FK + e)
                    nc.scalar.activation(HT[:, e, :], HT[:, e, :], ACT.Square).then_inc(kk_ready, 1)
                for b in range(GB):
                    k = O_FRV + 2 * b
                    ready(act, hb, k)
                    if b >= 2:
                        evacuated(act, hb, k - 3)
                    nc.scalar.activation(RR[b % 2], dense[k % 2][0:LQ, :], ACT.Sigmoid).then_inc(dense_free[k % 2], 1)

            def pre(g):
                hb = half_pre(g)
                ln_cols(hb, R_LN, "r_ln1_w", "r_ln1_b")
                ready(act, hb, R_W1)
                nc.scalar.activation(TA[:, :], dense[R_W1 % 2][:, 0:T], ACT.Tanh)
                nc.scalar.activation(TB[:, :], score[0][0:DM, 0:T], ACT.Tanh).then_inc(dense_free[R_W1 % 2], 1)
                ready(act, hb, TD1)
                nc.scalar.activation(TD, dense[TD1 % 2][0:DD, 0:T], ACT.Tanh).then_inc(dense_free[TD1 % 2], 1)
                for e in range(E):
                    k = TD2 + e
                    ready(act, hb, k)
                    nc.scalar.activation(HT[:, e, :], dense[k % 2][:, 0:T], ACT.Exp,
                                         bias=col("decay", e)).then_inc(dense_free[k % 2], 1)
                for e in range(E):
                    evacuated(act, hb, TD2 + e)
                    nc.scalar.activation(HT[:, e, :], HT[:, e, :], ACT.Exp, scale=-1.0).then_inc(decay_ready, 1)
                for j in (1, 2, 3):
                    for e in range(E):
                        k = P_AT[j] + e
                        ready(act, hb, k)
                        act.wait_ge(e_out[e], g * 64 + 16 * j)
                        nc.scalar.activation(HT[:, e, :], dense[k % 2][:, 0:T],
                                             ACT.Copy).then_inc(dense_free[k % 2], 1)
                for e in range(E):
                    k = P_AT[4] + e
                    ready(act, hb, k)
                    nc.scalar.activation(GT[:, e, :], dense[k % 2][:, 0:T], ACT.Silu).then_inc(dense_free[k % 2], 1)

            def step(g):
                first, last = isinstance(g, int) and g == 0, isinstance(g, int) and g == NG
                if last:
                    for b in range(GB):
                        for q in range(4):
                            repeat_decays(g - 1, b, q)
                else:
                    sequences(act, g, seq(not first))
                    mlp(g)
                if not first:
                    post(g)
                if not last:
                    pre(g)

            steps(act, step)

        @block.vector
        def _(dve):
            scan = Chain(dve, scan_chain)
            gn = Chain(dve, gn_chain)

            def row_stats(p, src, count):
                if count is not None:
                    dve.wait_ge(xn_ready[p], count - 1)
                apart(dve)
                nc.vector.bn_stats(bst[p][:, :], src).then_inc(stats_ready[p], 1)

            def row_var(p, count):
                dve.wait_ge(stats_ready[p], count)
                apart(dve)
                nc.vector.bn_aggr(mv[p][:, :], bst[p][:, :]).then_inc(var_ready[p], 1)

            def row_apply(p, src, par, count):
                dve.wait_ge(rstd_ready[p], count)
                nc.vector.tensor_scalar(xn[:, par, :], src, mv[p][:, 0:1], rstd[p][:, :],
                                        ALU.subtract, ALU.mult).then_inc(xn_ready[p], 1)

            def query(hb, k, half_):
                ready(dve, hb, k)
                nc.vector.tensor_tensor(qT[:, half_, :, :], dense[k % 2][:, 0:T].rearrange("p (e t) -> p e t", e=E),
                                        colb("q_b", LQ), ALU.add).then_inc(dense_free[k % 2], 1)

            dve.sem_inc(scan_step, 1)
            dve.wait_ge(x_in, 16)
            row_stats("seq", x_t[:, :], None)
            row_var("seq", 1)
            row_apply("seq", x_t[:, :], 0, 1)
            dve.wait_ge(cols_in, 16)
            query(0, PQ, 0)
            dve.wait_ge(params_in, 16 * PARAMS)

            def recurrence(gp, b, q, stage):
                i = b * 4 + q
                r, kk = rkw[:, q, 0, :], rkw[:, q, 1, :]
                if stage == 0:
                    scan.start((gp * RS + i) * CHANNEL)
                    if q == 0:
                        dve.wait_ge(rkw_in, channels_loaded(gp, b))
                    dve.wait_ge(scan_step, gp * RS + (i + 1))
                    scan.step(nc.vector.scalar_tensor_tensor(out=bon[:, 1, :], in0=r, scalar=ucol[:, bass.ds(i, 1)],
                                                             in1=kk, op0=ALU.mult, op1=ALU.mult))
                    scan.step(nc.vector.tensor_tensor(S[:, :, 1:LQ], VB[:, :, 0:LQ - 1],
                                                      kk[:, 0:LQ - 1].unsqueeze(1).to_broadcast([P, RS, LQ - 1]),
                                                      ALU.mult))
                    scan.step(nc.vector.tensor_copy(S[:, :, 0], s0[:, bass.ds(i, 1), :].rearrange("p a j -> p (a j)")))
                elif stage == 1:
                    scan.settle()
                    scan.step(nc.vector.tensor_tensor(bon[:, 0, :], bon[:, 0, :], bon[:, 1, :], ALU.add))
                    dve.wait_ge(wrep_ready, gp * RS + (i + 1))
                    for jh in range(RS // JH):
                        part = S[:, jh * JH:(jh + 1) * JH, :].rearrange("p j t -> p (j t)")
                        scan.step(nc.vector.tensor_tensor_scan(out=part, data0=wrep[:, q % 2, :], data1=part,
                                                               initial=0.0, op0=ALU.mult, op1=ALU.add))
                elif stage == 2:
                    scan.settle()
                    scan.step(nc.vector.tensor_tensor(S[:, :, :], S[:, :, :],
                                                      r.unsqueeze(1).to_broadcast([P, RS, LQ]), ALU.mult))
                else:
                    scan.settle()
                    nc.vector.tensor_tensor(YB[:, :, :], YB[:, :, :], S[:, :, :], ALU.add).then_inc(scan_step, 1)
                    scan.end(CHANNEL)

            def seq(with_scan):
                def body(g, b, par, n):
                    hb, nxt = half_seq(g, b), 1 - par

                    def normalise(k):
                        dve.wait_ge(pv_ready, n * H + 8 * (k + 1))
                        o = obank[k][0:LQ, 0:8 * (HD + 1)].rearrange("p (h d) -> p h d", h=8)
                        nc.vector.reciprocal(rden[:, 8 * k:8 * k + 8], o[:, :, HD]).then_inc(den_ready, 1)
                        dve.wait_ge(den_ready, n * 2 + (k + 1))
                        nc.vector.tensor_tensor(on[:, 256 * k:256 * (k + 1)].rearrange("p (h d) -> p h d", h=8),
                                                o[:, :, 0:HD],
                                                rden[:, 8 * k:8 * k + 8].unsqueeze(2).to_broadcast([LQ, 8, HD]),
                                                ALU.mult).then_inc(on_ready, 1)

                    dve.wait_ge(maskb_ready, n + 1)
                    for u in range(H):
                        dve.wait_ge(score_ready, n * H + (u + 1))
                        if u >= 2:
                            dve.wait_ge(prob_ready, n * H + (u - 1))
                        apart(dve)
                        nc.vector.tensor_tensor_reduce(
                            out=sm[:, u % 2, :], in0=score[u % 2][0:LQ, 0:LK], in1=maskb[:, :], scale=-SCALE,
                            scalar=3.0e38, op0=ALU.add, op1=ALU.min,
                            accum_out=nm[:, u % 2:u % 2 + 1]).then_inc(sm_ready, 1)
                        if u == 6:
                            dve.wait_ge(x_in, n * 16 + 32)
                            row_stats("seq", x_t[:, :], n * 2 + 2)
                            row_var("seq", n * 2 + 2)
                        elif u == 8:
                            row_apply("seq", x_t[:, :], 0, n * 2 + 2)
                        elif u == 10:
                            normalise(0)
                        elif u == 14:
                            query(hb, TQ, nxt)
                        if with_scan:
                            recurrence(g - 1, b, u // 4, u % 4)
                    normalise(1)
                    ready(dve, hb, TO)
                    nc.vector.tensor_tensor(onT[:, :, :], dense[TO % 2][:, 0:T].rearrange("p (e t) -> p e t", e=E),
                                            colb("v_b", LQ), ALU.add).then_inc(dense_free[TO % 2], 1)
                    ready(dve, hb, TC)
                    dve.wait_ge(res_ready, n + 1)
                    rows = X[:, (g % 2) * GB + b, :]
                    nc.vector.tensor_tensor(rows, dense[TC % 2][0:LQ, :], res[:, :], ALU.add
                                            ).then_inc(dense_free[TC % 2], 1)
                    evacuated(dve, hb, TC)
                    row_stats("seq", rows, n * 2 + 3)
                    row_var("seq", n * 2 + 3)
                    row_apply("seq", rows, 1, n * 2 + 3)
                return body

            def over_j(v):
                return v.unsqueeze(1).to_broadcast([P, RS, LQ])

            def group_norm(gp):
                GN = 7
                gn.start(gp * GN)
                dve.wait_ge(scan_step, gp * RS + (RS + 1))
                gn.step(nc.vector.tensor_tensor(VB[:, :, :], VB[:, :, :], over_j(bon[:, 0, :]), ALU.mult))
                gn.settle()
                gn.step(nc.vector.tensor_tensor(YB[:, :, :], YB[:, :, :], VB[:, :, :], ALU.add))
                gn.settle()
                gn.step(nc.vector.tensor_reduce(gst[:, 0, :], YB[:, :, :].rearrange("p j t -> p t j"),
                                                axis=AX.X, op=ALU.add))
                gn.settle()
                gn.step(nc.vector.tensor_scalar(gst[:, 0, :], gst[:, 0, :], 1.0 / RS, None, ALU.mult))
                gn.settle()
                gn.step(nc.vector.tensor_tensor(YB[:, :, :], YB[:, :, :], over_j(gst[:, 0, :]), ALU.subtract))
                gn.settle()
                gn.step(nc.vector.tensor_tensor(VB[:, :, :], YB[:, :, :], YB[:, :, :], ALU.mult))
                gn.settle()
                nc.vector.tensor_reduce(gst[:, 1, :], VB[:, :, :].rearrange("p j t -> p t j"),
                                        axis=AX.X, op=ALU.add).then_inc(var_ready["gn"], 1)
                dve.wait_ge(rstd_ready["gn"], gp + 1)
                nc.vector.tensor_tensor(YB[:, :, :], YB[:, :, :], over_j(gst[:, 2, :]), ALU.mult).then_inc(y_norm, 1)
                gn.step(nc.vector.memset(bon[:, 0, :], 0.0))
                gn.end(GN)

            def shift(p, which, gp):
                nc.vector.tensor_copy(XA[:, :, :, 0], shc[:, which, :, bass.ds(gp * GB, GB)]).then_inc(shift_ready[p], 1)
                dve.wait_ge(shift_ready[p], gp * 2 + 1)
                nc.vector.tensor_tensor(SX[:, :, :], XAc[:, :, 0:LQ], XAc[:, :, 1:LQ + 1],
                                        ALU.subtract).then_inc(shift_ready[p], 1)
                dve.wait_ge(shift_ready[p], gp * 2 + 2)

            def mix_with(dst, name):
                for e in range(E):
                    last_ = nc.vector.scalar_tensor_tensor(
                        out=dst[:, e, :].rearrange("p (b t) -> p b t", b=GB), in0=SX[:, GB * e:GB * (e + 1), :],
                        scalar=col(name, e), in1=XAs[:, e, :, :], op0=ALU.mult, op1=ALU.add)
                return last_

            def gate(g):
                dve.wait_ge(y_in, g * 64)
                for e in range(E):
                    last_ = nc.vector.tensor_scalar(C[0][:, e, :], C[0][:, e, :], col("gn_w", e), col("gn_b", e),
                                                    ALU.mult, ALU.add)
                last_.then_inc(gn_scaled, 1)
                dve.wait_ge(gn_scaled, g)
                nc.vector.tensor_tensor(C[0][:, :, :], C[0][:, :, :], GT[:, :, :], ALU.mult).then_inc(og_ready, 1)

            def mlp_bias(g):
                at = (g % 2) * GB
                rows = X[:, at:at + GB, :] if isinstance(g, int) else X[:, bass.ds(at, GB), :]
                dve.wait_ge(xn_ready["seq"], g * 8 + 9)
                nc.vector.tensor_tensor(rows, rows, pb[:, :].unsqueeze(1).to_broadcast([LQ, GB, D]),
                                        ALU.add).then_inc(bias_added, 1)
                dve.wait_ge(bias_added, g + 1)

            def mlp_add(g):
                for b in range(GB):
                    rows = X[:, (g % 2) * GB + b, :]
                    dve.wait_ge(acc_ready, g * GB + (b + 1))
                    nc.vector.tensor_tensor(rows, rows, acc[b][0:LQ, :], ALU.add).then_inc(x1_ready, 1)

            def post(g):
                hb = half_post(g)
                for b in range(GB):
                    k = O_OUT + b
                    count = (g - 1) * GB + (b + 1)
                    rows = X[:, ((g - 1) % 2) * GB + b, :]
                    ready(dve, hb, k)
                    nc.vector.tensor_tensor(rows, rows, dense[k % 2][0:LQ, :],
                                            ALU.add).then_inc(dense_free[k % 2], 1)
                    evacuated(dve, hb, k)
                    if b >= 2:
                        ready(dve, hb, O_LN + b - 2)
                    row_stats("post", rows, count if b else None)
                    row_var("post", count)
                    row_apply("post", rows, b % 2, count)
                evacuated(dve, hb, O_LN + 2)
                evacuated(dve, hb, O_LN + 3)
                shift("post", 0, g - 1)
                mix_with(C[0], "mix_k").then_inc(ck_ready, 1)
                mix_with(C[1], "mix_r").then_inc(ck_ready, 1)
                for b in range(GB):
                    k = O_FRV + 2 * b + 1
                    rows = X[:, ((g - 1) % 2) * GB + b, :]
                    evacuated(dve, hb, k - 1)
                    ready(dve, hb, k)
                    if b >= 2:
                        dve.wait_ge(out_ready, (g - 1) * GB + (b - 1))
                    nc.vector.tensor_tensor(xn[:, b % 2, :], dense[k % 2][0:LQ, :], RR[b % 2],
                                            ALU.mult).then_inc(dense_free[k % 2], 1)
                    evacuated(dve, hb, k)
                    nc.vector.tensor_tensor(rows, rows, xn[:, b % 2, :], ALU.add).then_inc(out_ready, 1)
                dve.wait_ge(out_ready, g * GB)

            def pre(g):
                hb = half_pre(g)
                for b in range(GB):
                    count = g * GB + (b + 1)
                    rows = X[:, (g % 2) * GB + b, :]
                    if b >= 2:
                        ready(dve, hb, R_LN + b - 2)
                    dve.wait_ge(x1_ready, count)
                    row_stats("pre", rows, count if b else None)
                    row_var("pre", count)
                    row_apply("pre", rows, b % 2, count)
                evacuated(dve, hb, R_LN + 2)
                evacuated(dve, hb, R_LN + 3)
                shift("pre", 1, g)
                mix_with(C[0], "maa_x").then_inc(mix_ready, 1)
                for j in range(5):
                    dst = C[j % 2]
                    for e in range(E):
                        k = X_AT[j] + e
                        ready(dve, hb, k)
                        nc.vector.scalar_tensor_tensor(
                            out=dst[:, e, :], in0=dense[k % 2][:, 0:T], scalar=col(f"maa_{ORDER[j]}", e),
                            in1=SX[:, GB * e:GB * (e + 1), :].rearrange("p b t -> p (b t)"),
                            op0=ALU.add, op1=ALU.mult).then_inc(dense_free[k % 2], 1)
                    for e in range(E):
                        evacuated(dve, hb, X_AT[j] + e)
                        last_ = nc.vector.tensor_tensor(dst[:, e, :].rearrange("p (b t) -> p b t", b=GB),
                                                        dst[:, e, :].rearrange("p (b t) -> p b t", b=GB),
                                                        XAs[:, e, :, :], ALU.add)
                    last_.then_inc(mix_ready, 1)
                if not (isinstance(g, int) and g == 0):
                    dve.wait_ge(out_done, g * 64)
                    apart(dve)
                nc.vector.memset(YB[:, :, :], 0.0).then_inc(yb_zero, 1)
                dve.wait_ge(yb_zero, g + 1)
                apart(dve)

            yb_zero = sem("yb_zero")
            nc.vector.memset(bon[:, 0, :], 0.0).then_inc(yb_zero, 1)
            dve.wait_ge(yb_zero, 1)
            dve.sem_clear(yb_zero)

            def step(g):
                first, last = isinstance(g, int) and g == 0, isinstance(g, int) and g == NG
                if not first:
                    dve.wait_ge(v_in, g * 80)
                    apart(dve)
                if not last:
                    sequences(dve, g, seq(not first))
                else:
                    with dve.Fori(0, GB) as b:
                        for q in range(4):
                            for stage in range(4):
                                recurrence(g - 1, b, q, stage)
                        apart(dve)
                if not first:
                    group_norm(g - 1)
                if not last:
                    mlp_bias(g)
                if not first:
                    gate(g)
                if not last:
                    mlp_add(g)
                if not first:
                    post(g)
                if not last:
                    pre(g)

            steps(dve, step)

        @block.tensor
        def _(pe):
            pe.sem_inc(dense_ready, READY0)
            for k in range(SLOTS):
                pe.sem_inc(ring_used[k], 1)

            def product(out_ap, pairs, lo=0, hi=None):
                hi = len(pairs) if hi is None else hi
                for k in range(lo, hi):
                    last_ = nc.tensor.matmul(out_ap, pairs[k][0], pairs[k][1], start=(k == 0),
                                             stop=(k == len(pairs) - 1))
                return last_

            def part(hb, k, out_ap, pairs, piece):
                if piece != 1:
                    bank_free(pe, hb, k)
                mid = len(pairs) // 2
                last_ = product(out_ap, pairs, mid if piece == 1 else 0, mid if piece == 0 else None)
                if piece != 0:
                    last_.then_inc(dense_ready, 1)

            def keys(hb, k, e, piece=None):
                part(hb, k, dense[k % 2][:, 0:LK],
                     [(Wk[:, c, e * P:(e + 1) * P], ctx_t[:, c, :]) for c in range(E)], piece)

            def values(hb, k, chunk, piece=None):
                part(hb, k, dense[k % 2][0:KW, :],
                     [(ctx_t[:, c, chunk * KW:(chunk + 1) * KW], Wv[:, c, :]) for c in range(E)], piece)

            def rows_to_cols(k, rows, es=range(E)):
                for at, e in enumerate(es):
                    last_ = nc.tensor.transpose(dense[k % 2][:, at * LQ:(at + 1) * LQ], rows[:, e * P:(e + 1) * P],
                                                ident[0:LQ, 0:LQ])
                last_.then_inc(dense_ready, 1)

            def query(k, es=range(E)):
                for e in es:
                    last_ = product(dense[k % 2][:, e * LQ:(e + 1) * LQ],
                                    [(Wq[:, c, e * P:(e + 1) * P], xnT[:, c, :]) for c in range(E)])
                if E - 1 in es:
                    last_.then_inc(dense_ready, 1)

            pe.wait_ge(ctx_in, 16)
            pe.wait_ge(wk_in, 16)
            for e in range(E):
                keys(0, PK + e, e)
            pe.wait_ge(wv_in, 16)
            values(0, PV0, 0)
            pe.wait_ge(consts_made, 5)
            pe.wait_ge(xn_ready["seq"], 1)
            for k, es in ((PXA, (0, 1)), (PXB, (2, 3))):
                bank_free(pe, 0, k)
                rows_to_cols(k, xn[:, 0, :], es)
            evacuated(pe, 0, PXA)
            evacuated(pe, 0, PXB)
            pe.wait_ge(wq_in, 16)
            query(PQ)
            values(0, PV1, 1)
            values(0, PV2, 2)
            pe.wait_ge(params_in, 16 * PARAMS)
            evacuated(pe, 0, PQ)
            evacuated(pe, 0, PV1)
            evacuated(pe, 0, PV2)

            def seq(g, b, par, n):
                hb = half_seq(g, b)

                def scores(u):
                    if u >= 2:
                        pe.wait_ge(sm_ready, n * H + (u - 1))
                    r = HD * (u % 4)
                    nc.tensor.matmul(score[u % 2][0:LQ, 0:LK], qT[r:r + HD, par, u // 4, :],
                                     KT[r:r + HD, par, u // 4, :], start=True, stop=True).then_inc(score_ready, 1)

                def turn(u):
                    pe.wait_ge(prob_ready, n * H + (u + 1))
                    if u >= 2:
                        pe.wait_ge(probT_ready, n * H + (u - 1))
                    for k in range(KC):
                        last_ = nc.tensor.transpose(pT[u % 2][0:KW, k * LQ:(k + 1) * LQ],
                                                    prob[:, u % 2, k * KW:(k + 1) * KW], ident[0:LQ, 0:LQ])
                    last_.then_inc(pT_ready, 1)

                def weigh(u):
                    pe.wait_ge(probT_ready, n * H + (u + 1))
                    at = (u % 8) * (HD + 1)
                    product(obank[u // 8][0:LQ, at:at + HD + 1],
                            [(probT[:, u % 2, k * LQ:(k + 1) * LQ], V[:, par, k, u, :]) for k in range(KC)]
                            ).then_inc(pv_ready, 1)

                scores(0)
                scores(1)
                for u in range(H):
                    if u + 2 < H:
                        scores(u + 2)
                    if u == 0:
                        pe.wait_ge(ctx_in, n * 16 + 32)
                    if u < 8:
                        keys(hb, TK + u // 2, u // 2, u % 2)
                    elif u in (8, 9):
                        values(hb, TV0, 0, u % 2)
                    elif u == 10:
                        pe.wait_ge(xn_ready["seq"], n * 2 + 2)
                        bank_free(pe, hb, TX)
                        rows_to_cols(TX, xn[:, 0, :])
                    elif u == 12:
                        evacuated(pe, hb, TX)
                        bank_free(pe, hb, TQ)
                        query(TQ, (0, 1))
                    elif u == 13:
                        query(TQ, (2, 3))
                    elif u == 15:
                        values(hb, TV1, 1, 0)
                    turn(u)
                    if u >= 1:
                        weigh(u - 1)
                weigh(H - 1)
                values(hb, TV1, 1, 1)
                pe.wait_ge(on_ready, n * 2 + 2)
                bank_free(pe, hb, TO)
                rows_to_cols(TO, on)
                evacuated(pe, hb, TO)
                bank_free(pe, hb, TC)
                product(dense[TC % 2][0:LQ, :], [(onT[:, c, :], Wc[:, c, :]) for c in range(E)]
                        ).then_inc(dense_ready, 1)
                values(hb, TV2, 2)
                pe.wait_ge(xn_ready["seq"], n * 2 + 3)
                bank_free(pe, hb, TY)
                rows_to_cols(TY, xn[:, 1, :])
                evacuated(pe, hb, TV1)
                evacuated(pe, hb, TV2)

            def weights(g, k):
                pe.wait_ge(ring_in[k % SLOTS], (half_piece(g) + (k // SLOTS + 1)) * 16)
                return ring[:, k % SLOTS, :, :]

            def channels_out(hb, first_tile, w, src):
                for e in range(E):
                    k = first_tile + e
                    bank_free(pe, hb, k)
                    product(dense[k % 2][:, 0:T], [(w[:, c, e * P:(e + 1) * P], src[:, c, :]) for c in range(E)]
                            ).then_inc(dense_ready, 1)

            def used(k, hb, tile):
                ready(pe, hb, tile)
                pe.sem_inc(ring_used[k % SLOTS], 1)

            def mlp(g):
                hb = half_mlp(g)
                bank_free(pe, hb, 1)
                for m in range(4):
                    w = weights(g, 2 * m)
                    channels_out(hb, 4 * m, w, YT)
                    used(2 * m, hb, 4 * m + 3)
                    w = weights(g, 2 * m + 1)
                    evacuated(pe, hb, 4 * m + 2)
                    evacuated(pe, hb, 4 * m + 3)
                    for b in range(GB):
                        for c in range(E):
                            last_ = nc.tensor.matmul(acc[b][0:LQ, :], HT[:, c, b * LQ:(b + 1) * LQ], w[:, c, :],
                                                     start=(m == 0 and c == 0), stop=(m == 3 and c == E - 1))
                        if m == 3:
                            last_.then_inc(acc_ready, 1)
                    if m < 3:
                        last_.then_inc(mlp_used, 1)
                        pe.wait_ge(mlp_used, g * 3 + (m + 1))
                    else:
                        pe.wait_ge(acc_ready, g * GB + GB)
                    pe.sem_inc(ring_used[1], 1)

            def post(g):
                hb, gp = half_post(g), g - 1
                first_w = 0 if isinstance(g, int) and g == NG else 8
                w = weights(g, first_w)
                pe.wait_ge(og_ready, g)
                for b in range(GB):
                    k = O_OUT + b
                    bank_free(pe, hb, k)
                    product(dense[k % 2][0:LQ, :], [(C[0][:, c, b * LQ:(b + 1) * LQ], w[:, c, :]) for c in range(E)]
                            ).then_inc(dense_ready, 1)
                used(first_w, hb, O_OUT + 3)
                for b in range(GB):
                    pe.wait_ge(xn_ready["post"], gp * GB + (b + 1))
                    bank_free(pe, hb, O_LN + b)
                    rows_to_cols(O_LN + b, xn[:, b % 2, :])
                w = weights(g, first_w + 1)
                pe.wait_ge(ck_ready, gp * 2 + 1)
                channels_out(hb, O_FK, w, C[0])
                used(first_w + 1, hb, O_FK + 3)
                wr = weights(g, first_w + 2)
                wfv = weights(g, first_w + 3)
                pe.wait_ge(ck_ready, gp * 2 + 2)
                for b in range(GB):
                    k = O_FRV + 2 * b
                    bank_free(pe, hb, k)
                    product(dense[k % 2][0:LQ, :], [(C[1][:, c, b * LQ:(b + 1) * LQ], wr[:, c, :]) for c in range(E)]
                            ).then_inc(dense_ready, 1)
                    if b == 0:
                        pe.wait_ge(kk_ready, gp * E + E)
                    bank_free(pe, hb, k + 1)
                    product(dense[(k + 1) % 2][0:LQ, :],
                            [(HT[:, c, b * LQ:(b + 1) * LQ], wfv[:, c, :]) for c in range(E)]
                            ).then_inc(dense_ready, 1)
                used(first_w + 2, hb, O_FRV + 7)
                used(first_w + 3, hb, O_FRV + 7)

            def pre(g):
                hb = half_pre(g)
                first_w = 8 if isinstance(g, int) and g == 0 else 12
                for b in range(GB):
                    pe.wait_ge(xn_ready["pre"], g * GB + (b + 1))
                    bank_free(pe, hb, R_LN + b)
                    rows_to_cols(R_LN + b, xn[:, b % 2, :])
                pe.wait_ge(mix_ready, g * 6 + 1)
                bank_free(pe, hb, R_W1)
                product(dense[R_W1 % 2][:, 0:T], [(mw1[:, c, 0:P], C[0][:, c, :]) for c in range(E)])
                product(score[0][0:DM, 0:T], [(mw1[:, c, P:5 * DM], C[0][:, c, :]) for c in range(E)]
                        ).then_inc(dense_ready, 1)

                def low_rank(j):
                    q = ORDER[j]
                    w, a = (mw2b, TB[:, :]) if q == 4 else (mw2[DM * q:DM * (q + 1), :], TA[DM * q:DM * (q + 1), :])
                    for e in range(E):
                        k = X_AT[j] + e
                        bank_free(pe, hb, k)
                        nc.tensor.matmul(dense[k % 2][:, 0:T], w[:, e * P:(e + 1) * P], a,
                                         start=True, stop=True).then_inc(dense_ready, 1)

                evacuated(pe, hb, R_W1)
                low_rank(0)
                low_rank(1)
                pe.wait_ge(mix_ready, g * 6 + 2)
                bank_free(pe, hb, TD1)
                product(dense[TD1 % 2][0:DD, 0:T], [(tw1[:, c, :], C[0][:, c, :]) for c in range(E)]
                        ).then_inc(dense_ready, 1)
                evacuated(pe, hb, TD1)
                for e in range(E):
                    k = TD2 + e
                    bank_free(pe, hb, k)
                    nc.tensor.matmul(dense[k % 2][:, 0:T], tw2[:, e * P:(e + 1) * P], TD,
                                     start=True, stop=True).then_inc(dense_ready, 1)
                for j in range(2, 6):
                    if j < 5:
                        low_rank(j)
                    w = weights(g, first_w + j - 2)
                    pe.wait_ge(mix_ready, g * 6 + (j + 1))
                    channels_out(hb, P_AT[j - 1], w, C[(j - 1) % 2])
                    used(first_w + j - 2, hb, P_AT[j - 1] + 3)

            def step(g):
                first, last = isinstance(g, int) and g == 0, isinstance(g, int) and g == NG
                if not last:
                    sequences(pe, g, seq)
                    mlp(g)
                if not first:
                    post(g)
                if not last:
                    pre(g)

            steps(pe, step)


def kernel(x, ctx_2048, mask_BxS2_bf1, **p):
    import concourse.bacc as bacc
    from concourse.bass_utils import run_bass_kernel_spmd

    a = {k: np.asarray(v) for k, v in p.items()}
    x, ctx, mask = np.asarray(x), np.asarray(ctx_2048), np.asarray(mask_BxS2_bf1)
    l0 = {k[len("L0_xattn_"):]: v for k, v in a.items() if k.startswith("L0_xattn_")}
    l1 = {k[len("L1_xattn_"):]: v for k, v in a.items() if k.startswith("L1_xattn_")}
    vecs = [l0["ln1_w"], l0["ln1_b"], l0["q_b"], l0["k_b"], l0["v_b"], l0["ln2_w"], l0["ln2_b"],
            l1["ln1_w"], l1["ln1_b"], l1["ln2_w"], l1["ln2_b"], l1["maa_x"],
            *[l1["maa_stack"][0, j] for j in range(5)], l1["time_decay"], l1["gn_w"], l1["gn_b"],
            l1["ffn_maa_k"], l1["ffn_maa_r"], l0["fc_b"]]
    cols = np.concatenate([v.reshape(-1, P).T for v in vecs], axis=1)
    pieces = []
    for m in range(4):
        pieces += [l0["fc_w"][:, m * D:(m + 1) * D], l0["proj_w"][m * D:(m + 1) * D, :]]
    pieces += [l1[w].T for w in ("Wk", "Wv", "Wr", "Wg", "Wo", "Wfk", "Wfr", "Wfv")]
    arrays = {
        "x": x,
        "ctxT": ctx.transpose(0, 2, 1),
        "ctx": ctx,
        "mask": mask.view(np.uint8),
        "shiftcols": ctx[:, 0:2, :].reshape(B, 2, E, P).transpose(3, 1, 2, 0),
        "cols": cols,
        "wq": l0["q_w"], "wk": l0["k_w"], "wv": l0["v_w"], "wc": l0["cproj_w"],
        "cproj_b": l0["cproj_b"], "proj_b": l0["proj_b"],
        "stream": np.stack(pieces),
        "maa_w1": l1["maa_w1"], "maa_w2": l1["maa_w2"].reshape(5 * DM, D),
        "td_w1": l1["td_w1"], "td_w2": l1["td_w2"],
        "u": np.tile(l1["u"].reshape(RH, RS), (GB, 1)),
    }
    arrays = {f"in_{k}": np.ascontiguousarray(v) for k, v in arrays.items()}
    nc = bacc.Bacc("TRN2", target_bir_lowering=False, num_devices=1)
    args = [nc.dram_tensor(k, v.shape, mybir.dt.from_np(v.dtype), kind="ExternalInput").ap()
            for k, v in arrays.items()]
    out = nc.dram_tensor("out", (B, LQ, D), F32, kind="ExternalOutput").ap()
    build(nc, *args, out)
    r = run_bass_kernel_spmd(nc, [arrays], core_ids=[0])
    return r.results[0]["out"]
```

```python
import numpy as np
import concourse.bass as bass
import concourse.mybir as mybir
from contextlib import ExitStack

F32 = mybir.dt.float32
U8 = mybir.dt.uint8
ALU = mybir.AluOpType
ACT = mybir.ActivationFunctionType
AX = mybir.AxisListType

B, LQ, LK, D = 16, 112, 375, 512
P = 128
E = D // P
H, HD = 16, 32
INNER = 4 * D
GB = 4
NG = B // GB
T = GB * LQ
KC = 3
KW = LK // KC
RH, RS = 32, 16
JH = 8
DM, DD = 32, 64
EPS = 1e-5
SCALE = float(np.float32(1.0) / np.sqrt(np.float32(HD)))
BIG = float(2.0 ** 126)
SLOTS = 2

COLS = ["ln1_w", "ln1_b", "q_b", "k_b", "v_b", "ln2_w", "ln2_b",
        "r_ln1_w", "r_ln1_b", "r_ln2_w", "r_ln2_b", "maa_x",
        "maa_0", "maa_1", "maa_2", "maa_3", "maa_4", "decay", "gn_w", "gn_b", "mix_k", "mix_r"]
FCB = E * len(COLS)
NCOL = FCB + INNER // P
ORDER = [1, 0, 2, 3, 4]

TK, TV0, TX, TQ, TV1, TO, TC, TV2, TY = 0, 4, 5, 6, 7, 8, 9, 10, 11
SEQ_TILES = 12
PK, PV0, PXA, PXB, PQ, PV1, PV2 = 0, 4, 5, 6, 7, 8, 9
FIRST_TILES = 10
MLP_TILES = 16
POST_TILES = 20
O_OUT, O_LN, O_FK = 0, 4, 8
PRE_TILES = 46
R_LN, R_W1 = 0, 4
X_AT = [5, 9, 18, 26, 34]
TD1, TD2 = 13, 14
P_AT = [None, 22, 30, 38, 42]
READY0 = 1

STEP0 = GB * SEQ_TILES + MLP_TILES + PRE_TILES
STEP = STEP0 + POST_TILES
W_MLP, W_OUT, W_PROJ = range(0, 8), range(12, 16), range(8, 12)


def half_step(g):
    return FIRST_TILES // 2 if isinstance(g, int) and g == 0 else g * (STEP // 2) + (FIRST_TILES + STEP0 - STEP) // 2


def half_seq(g, b):
    return half_step(g) + b * (SEQ_TILES // 2)


def half_mlp(g):
    return half_step(g) + GB * SEQ_TILES // 2


def half_post(g):
    return half_step(g) if isinstance(g, int) and g == NG else half_mlp(g) + MLP_TILES // 2


def half_pre(g):
    first = isinstance(g, int) and g == 0
    return half_mlp(g) + (MLP_TILES + (0 if first else POST_TILES)) // 2


def frv_at(g):
    return 12 if isinstance(g, int) and g == NG else 16


def ln_tiles(g):
    return (half_pre(g), R_LN) if isinstance(g, int) and g == 0 else (half_post(g), 12)


def pieces_of(g):
    first, last = isinstance(g, int) and g == 0, isinstance(g, int) and g == NG
    return [*([] if last else W_MLP), *([] if first else W_OUT), *([] if last else W_PROJ)]


def half_piece(g):
    return 0 if isinstance(g, int) and g == 0 else g * 8 - 2


class Chain:

    def __init__(self, engine, sem):
        self.engine, self.sem, self.base, self.count = engine, sem, 0, 0

    def start(self, base):
        self.base, self.count = base, 0

    def step(self, instruction):
        self.count += 1
        instruction.then_inc(self.sem, 1)

    def settle(self):
        self.engine.wait_ge(self.sem, self.base + self.count)

    def end(self, count):
        assert self.count == count, (self.count, count)


def build(nc, x, ctxT, ctx, mask, shiftcols, cols, wq, wk, wv, wc, cproj_b, proj_b, stream,
          maa_w1, maa_w2, td_w1, td_w2, u, out):
    rkw_d = nc.dram_tensor("rkw_scratch", (B * RH, RS, 3, LQ), F32, kind="Internal").ap()
    v_d = nc.dram_tensor("v_scratch", (B * RH, RS * LQ), F32, kind="Internal").ap()
    y_d = nc.dram_tensor("y_scratch", (B * RH, RS * LQ), F32, kind="Internal").ap()

    ctxm = ExitStack()
    with ctxm:
        def sb(name, shape, dt=F32):
            return ctxm.enter_context(nc.sbuf_tensor(name, shape, dt))

        def sem(name):
            return ctxm.enter_context(nc.semaphore(name))

        ident = sb("ident", [P, P])
        colt = sb("colt", [P, NCOL])
        Wq, Wk, Wv, Wc = (sb(n, [P, E, D]) for n in ("Wq", "Wk", "Wv", "Wc"))
        ring = sb("ring", [P, SLOTS, E, D])
        mw1 = sb("mw1", [P, E, 5 * DM])
        mw2 = sb("mw2", [P, D])
        mw2b = sb("mw2b", [DM, D])
        tw1 = sb("tw1", [P, E, DD])
        tw2 = sb("tw2", [DD, D])
        cb = sb("cb", [LQ, D])
        pb = sb("pb", [LQ, D])
        shc = sb("shc", [P, 2, E, B])
        ucol = sb("ucol", [P, RS])
        half = sb("half", [P, 1])
        eps_col = sb("eps_col", [P, 1])
        ctx_t = sb("ctx_t", [P, E, LK])
        x_t = sb("x_t", [LQ, D])
        res = sb("res", [LQ, D])
        xn = sb("xn", [LQ, 2, D])
        xnT = sb("xnT", [P, E, LQ])
        qT = sb("qT", [P, 2, E, LQ])
        KT = sb("KT", [P, 2, E, LK])
        V = sb("V", [KW, 2, KC, H, HD + 1])
        mrow = sb("mrow", [LQ, LK], U8)
        maskb = sb("maskb", [LQ, LK])
        sm = sb("sm", [LQ, 2, LK])
        nm = sb("nm", [LQ, 2])
        prob = sb("prob", [LQ, 2, LK])
        probT = sb("probT", [KW, 2, KC * LQ])
        rden = sb("rden", [LQ, H])
        on = sb("on", [LQ, D])
        onT = sb("onT", [P, E, LQ])
        PH = ("seq", "pre", "post")
        bst = {p: sb(f"bst_{p}", [LQ, GB, 6]) for p in PH}
        mv = {p: sb(f"mv_{p}", [LQ, GB, 2]) for p in PH}
        vare = {p: sb(f"vare_{p}", [LQ, GB]) for p in PH}
        rstd = {p: sb(f"rstd_{p}", [LQ, GB]) for p in PH}
        X = sb("X", [LQ, 2 * GB, D])
        XA = sb("XA", [P, E, GB, LQ + 1])
        SX = sb("SX", [P, E * GB, LQ])
        C = [sb("C0", [P, E, T]), sb("C1", [P, E, T])]
        HT = sb("HT", [P, E, T])
        GT = sb("GT", [P, E, T])
        TA = sb("TA", [P, T])
        TB = sb("TB", [DM, T])
        VB = sb("VB", [P, RS, LQ])
        YB = sb("YB", [P, RS, LQ])
        rkw = sb("rkw", [P, 4, 3, LQ])
        s0 = sb("s0", [P, RS, RS])
        bon = sb("bon", [P, 2, LQ])
        gst = sb("gst", [P, 3, LQ])

        YT = SX[:, :, :].rearrange("p (e b) t -> p e (b t)", e=E)
        TD = GT[0:DD, 0, :]
        RR = [GT[0:LQ, :, :].rearrange("p e t -> p (e t)")[:, k * D:(k + 1) * D] for k in range(2)]
        XAs = XA[:, :, :, 1:LQ + 1]
        XAc = XA[:, :, :, :].rearrange("p e b t -> p (e b) t")
        S = C[1][:, :, :].rearrange("p e (b t) -> p (e b) t", b=GB)
        wrep = XA[:, :, :, :].rearrange("p e b t -> p (e b t)")[:, 0:2 * JH * LQ].rearrange(
            "p (s n) -> p s n", s=2)

        bank = [ctxm.enter_context(nc.psum_tensor(f"bank{k}", [P, 512], F32)) for k in range(8)]
        dense = bank[0:2]
        score = bank[2:4]
        pT = bank[4:6]
        obank = bank[6:8]
        acc = [score[0], score[1], pT[0], pT[1]]

        def col(name, e):
            k = COLS.index(name) * E + e
            return colt[:, k:k + 1]

        def colb(name, n):
            k = COLS.index(name) * E
            return colt[:, k:k + E].unsqueeze(2).to_broadcast([P, E, n])

        wk_in, wv_in, wq_in, cols_in = sem("wk_in"), sem("wv_in"), sem("wq_in"), sem("cols_in")
        params_in = sem("params_in")
        consts_made = sem("consts_made")
        ring_in = [sem(f"ring_in{k}") for k in range(SLOTS)]
        ring_used = [sem(f"ring_used{k}") for k in range(SLOTS)]
        x_in, ctx_in, mask_in = sem("x_in"), sem("ctx_in"), sem("mask_in")
        res_ready = sem("res_ready")
        maskb_ready = sem("maskb_ready")
        stats_ready = {p: sem(f"stats_ready_{p}") for p in PH}
        var_ready = {p: sem(f"var_ready_{p}") for p in (*PH, "gn")}
        rstd_ready = {p: sem(f"rstd_ready_{p}") for p in (*PH, "gn")}
        eps_added = {p: sem(f"eps_added_{p}") for p in PH}
        xn_ready = {p: sem(f"xn_ready_{p}") for p in PH}
        dense_ready = sem("dense_ready")
        dense_free = [sem("dense_free0"), sem("dense_free1")]
        score_ready = sem("score_ready")
        sm_ready = sem("sm_ready")
        prob_ready = sem("prob_ready")
        pT_ready = sem("pT_ready")
        probT_ready = sem("probT_ready")
        pv_ready = sem("pv_ready")
        den_ready = sem("den_ready")
        on_ready = sem("on_ready")
        mlp_used = sem("mlp_used")
        acc_ready = sem("acc_ready")
        bias_added = sem("bias_added")
        x1_ready = sem("x1_ready")
        mix_ready = sem("mix_ready")
        shift_ready = {p: sem(f"shift_ready_{p}") for p in ("pre", "post")}
        gn_scaled = sem("gn_scaled")
        og_ready = sem("og_ready")
        ck_ready = sem("ck_ready")
        decay_ready = sem("decay_ready")
        e_out = [sem(f"e_out{k}") for k in range(E)]
        v_in = sem("v_in")
        rkw_in = sem("rkw_in")
        wrep_ready = sem("wrep_ready")
        scan_chain = sem("scan_chain")
        scan_step = sem("scan_step")
        gn_chain = sem("gn_chain")
        bon_zero, yb_zero = sem("bon_zero"), sem("yb_zero")
        y_norm = sem("y_norm")
        y_out, y_in = sem("y_out"), sem("y_in")
        kk_ready = sem("kk_ready")
        out_ready = sem("out_ready")
        out_done = sem("out_done")
        carried = sem("carried")

        def apart(eng):
            eng.sem_inc(carried, 1)

        def ready(eng, hb, k):
            eng.wait_ge(dense_ready, 2 * hb + (READY0 + k + 1))

        def evacuated(eng, hb, k):
            eng.wait_ge(dense_free[k % 2], hb + (k // 2 + 2))

        def bank_free(eng, hb, k):
            eng.wait_ge(dense_free[k % 2], hb + (k // 2 + 1))

        PARAMS = 11
        CHANNEL = 7
        PAIRS = GB // 2

        def steps(eng, step):
            step(0)
            with eng.Fori(1, NG) as g:
                step(g)
            step(NG)

        def sequences(eng, g, seq):
            with eng.Fori(0, PAIRS) as bp:
                for par in range(2):
                    b = bp * 2 + par
                    seq(g, b, par, g * GB + b)

        rkw_last = [rkw, *(w[:, :, :].rearrange("p c n -> p (c n)")[:, 0:4 * 3 * LQ].rearrange(
            "p (q s t) -> p q s t", q=4, s=3) for w in (Wk, Wv, Wq))]
        S_last = [S, C[0][:, :, :].rearrange("p e (b t) -> p (e b) t", b=GB), SX,
                  HT[:, :, :].rearrange("p e (b t) -> p (e b) t", b=GB)]
        rkw_last_in = [sem(f"rkw_last_in{b}") for b in range(GB)]
        kv_ready = sem("kv_ready")
        summed = sem("summed")

        block = ctxm.enter_context(nc.Block())

        def channels_loaded(gp, b):
            return gp * 160 + b * 32 + 32

        def last_loaded(eng, b):
            eng.wait_ge(rkw_last_in[b], 32)

        def load_channels(eng, gp, b, rkw=rkw, done=rkw_in):
            rows = rkw_d[bass.ds(gp * P, P), bass.ds(b * 4, 4), :, :]
            eng.dma_start(rkw[:, :, 0:2, :].rearrange("p q s t -> p q (s t)"),
                          rows[:, :, 0:2, :].rearrange("p q s t -> p q (s t)")).then_inc(done, 16)
            eng.dma_start(rkw[:, :, 2, 1:LQ], rows[:, :, 2, 0:LQ - 1]).then_inc(done, 16)

        @block.sync
        def _(sp):
            def load_ctx(n):
                sp.dma_start(ctx_t[:, :, :], ctxT[n % B, :, :].rearrange("(c p) t -> p c t", p=P)).then_inc(ctx_in, 16)

            def load_x(n):
                sp.dma_start(x_t[:, :], x[n % B, :, :]).then_inc(x_in, 16)

            def load_mask(n):
                sp.dma_start(mrow[:, :], mask[n % B, :].partition_broadcast(LQ)).then_inc(mask_in, 16)

            load_x(0)
            load_ctx(0)
            sp.dma_start(Wk[:, :, :], wk.rearrange("(c p) n -> p c n", p=P)).then_inc(wk_in, 16)
            sp.dma_start(Wv[:, :, :], wv.rearrange("(c p) n -> p c n", p=P)).then_inc(wv_in, 16)
            load_mask(0)
            sp.wait_ge(res_ready, 1)
            sp.wait_ge(xn_ready["seq"], 1)
            load_x(1)
            sp.wait_ge(maskb_ready, 1)
            load_mask(1)
            ready(sp, 0, PV2)
            load_ctx(1)

            def seq(g, b, par, n):
                ready(sp, half_seq(g, b), TV2)
                load_ctx(n + 2)
                sp.wait_ge(res_ready, n + 2)
                sp.wait_ge(xn_ready["seq"], n * 2 + 2)
                load_x(n + 2)
                sp.wait_ge(maskb_ready, n + 2)
                apart(sp)
                load_mask(n + 2)

            def step(g):
                first, last = isinstance(g, int) and g == 0, isinstance(g, int) and g == NG
                order = pieces_of(g)

                def piece(k):
                    sp.wait_ge(ring_used[k % SLOTS], half_piece(g) + (k // SLOTS + 1))
                    sp.dma_start(ring[:, k % SLOTS, :, :],
                                 stream[order[k]].rearrange("(c p) n -> p c n", p=P)).then_inc(ring_in[k % SLOTS], 16)

                if not first:
                    for e in range(E):
                        sp.wait_ge(e_out[e], g * 64)
                    sp.dma_start(VB[:, :, :].rearrange("p j t -> p (j t)"),
                                 v_d[bass.ds((g - 1) * P, P), :]).then_inc(v_in, 16)
                    if last:
                        load_channels(sp, g - 1, 0, rkw, rkw_last_in[0])
                    for b in range(GB):
                        sp.dma_start(s0[RH * b:RH * (b + 1), :, :].rearrange("p i j -> p (i j)"),
                                     ctx[(g - 1) * GB + b, 2:2 + RS, :].rearrange("s (q c) -> (s q) c", c=RS * RS)
                                     ).then_inc(v_in, 16)
                    if last:
                        for b in range(1, GB):
                            load_channels(sp, g - 1, b, rkw_last[b], rkw_last_in[b])
                piece(0)
                piece(1)
                if not last:
                    sequences(sp, g, seq)
                if not last:
                    piece(2)
                if not first:
                    sp.wait_ge(y_norm, g)
                    sp.dma_start(y_d[bass.ds((g - 1) * P, P), :],
                                 YB[:, :, :].rearrange("p j t -> p (j t)")).then_inc(y_out, 16)
                    sp.wait_ge(y_out, g * 16)
                    for b in range(GB):
                        sp.dma_start(C[0][:, :, b * LQ:(b + 1) * LQ],
                                     y_d[bass.ds((g - 1) * P + RH * b, RH), :].rearrange("h (j t) -> (h j) t", t=LQ)
                                     .rearrange("(e p) t -> p e t", p=P)).then_inc(y_in, 16)
                for k in range(2 if last else 3, len(order)):
                    piece(k)

            steps(sp, step)
            sp.wait_ge(out_done, 16 * B)
            sp.wait_ge(x_in, 16 * (B + 2))
            sp.wait_ge(ctx_in, 16 * (B + 2))
            sp.wait_ge(mask_in, 16 * (B + 2))

        @block.gpsimd
        def _(pool):
            nc.gpsimd.memset(ident[:, :], 0.0).then_inc(consts_made, 1)
            nc.gpsimd.memset(half[:, :], -0.5).then_inc(consts_made, 1)
            nc.gpsimd.memset(eps_col[:, :], EPS).then_inc(consts_made, 1)
            nc.gpsimd.memset(rkw[:, :, 2, 0:1], 0.0).then_inc(consts_made, 1)
            nc.gpsimd.memset(V[:, :, :, :, HD:HD + 1], 1.0).then_inc(consts_made, 1)
            pool.wait_ge(consts_made, 5)
            nc.gpsimd.affine_select(out=ident[:, :], in_=ident[:, :], compare_op=ALU.not_equal, fill=1.0,
                                    base=0, pattern=[[-1, P]], channel_multiplier=1).then_inc(consts_made, 1)

            def inv_std(p, count, slot=0):
                pool.wait_ge(var_ready[p], count)
                apart(pool)
                at = slice(slot, slot + 1)
                nc.gpsimd.tensor_scalar(vare[p][:, at], mv[p][:, slot, 1:2], EPS, None, ALU.add
                                        ).then_inc(eps_added[p], 1)
                pool.wait_ge(eps_added[p], count)
                nc.gpsimd.tensor_tensor(rstd[p][:, at], vare[p][:, at], half[0:LQ, :], ALU.pow
                                        ).then_inc(rstd_ready[p], 1)

            def residual(n):
                pool.wait_ge(x_in, n * 16 + 16)
                nc.gpsimd.tensor_tensor(res[:, :], x_t[:, :], cb[:, :], ALU.add).then_inc(res_ready, 1)

            def mask_rows(n):
                pool.wait_ge(mask_in, n * 16 + 16)
                apart(pool)
                nc.gpsimd.tensor_scalar(maskb[:, :], mrow[:, :], BIG, -BIG, ALU.mult, ALU.add).then_inc(maskb_ready, 1)

            inv_std("seq", 1)
            pool.wait_ge(params_in, 16 * PARAMS)
            residual(0)
            mask_rows(0)

            def seq(scan):
                def body(g, b, par, n):
                    inv_std("seq", n * 2 + 2)
                    if scan:
                        pool.wait_ge(scan_step, (g - 1) * RS + b * 4 + 5)
                        load_channels(pool, g - 1, (b + 1) % GB)
                    inv_std("seq", n * 2 + 3)
                    evacuated(pool, half_seq(g, b), TC)
                    mask_rows(n + 1)
                    residual(n + 1)
                return body

            def step(g):
                first, last = isinstance(g, int) and g == 0, isinstance(g, int) and g == NG
                if not first:
                    for e in range(E):
                        pool.wait_ge(e_out[e], g * 64)
                    if not last:
                        load_channels(pool, g - 1, 0)
                if not last:
                    sequences(pool, g, seq(not first))
                else:
                    ready(pool, half_pre(g - 1), TD1)
                    for b in range(1, GB):
                        nc.gpsimd.memset(rkw_last[b][:, :, 2, 0:1], 0.0).then_inc(consts_made, 1)
                    ready(pool, half_pre(g - 1), P_AT[4] + 3)
                    pool.wait_ge(v_in, g * 80)
                    for i in range(RS):
                        b, q = i // 4, i % 4
                        if q == 0:
                            last_loaded(pool, b)
                        if i >= 4:
                            pool.wait_ge(summed, i - 3)
                        nc.gpsimd.tensor_tensor(
                            S_last[q][:, :, 1:LQ], VB[:, :, 0:LQ - 1],
                            rkw_last[b][:, q, 1, 0:LQ - 1].unsqueeze(1).to_broadcast([P, RS, LQ - 1]),
                            ALU.mult).then_inc(kv_ready, 1)
                        pool.wait_ge(kv_ready, 2 * i + 1)
                        nc.gpsimd.tensor_tensor(rkw_last[b][:, q, 1, :], rkw_last[b][:, q, 0, :],
                                                rkw_last[b][:, q, 1, :], ALU.mult).then_inc(kv_ready, 1)
                if not first:
                    if not last:
                        pool.wait_ge(rkw_in, g * 160)
                    for b in range(GB):
                        inv_std("post", (g - 1) * GB + (b + 1), b)
                        if not last:
                            inv_std("pre", g * GB + (b + 1), b)
                    for b in range(GB):
                        pool.wait_ge(out_ready, (g - 1) * GB + (b + 1))
                        pool.dma_start(out[(g - 1) * GB + b, :, :],
                                       X[:, ((g - 1) % 2) * GB + b, :]).then_inc(out_done, 16)
                if last:
                    return
                if first:
                    for b in range(GB):
                        inv_std("pre", g * GB + (b + 1), b)
                hb = half_pre(g)

                def store(which, e):
                    rows = bass.ds(g * P, P)
                    if which == 3:
                        dst = v_d[rows, :].rearrange("(b h) (j t) -> b (h j) t", b=GB, t=LQ)[:, e * P:(e + 1) * P, :]
                    else:
                        dst = rkw_d[rows, :, :, :].rearrange("(b h) i s t -> b (h i) s t", b=GB)[
                            :, e * P:(e + 1) * P, which, :]
                    pool.dma_start(dst.rearrange("b p t -> p b t"),
                                   HT[:, e, :].rearrange("p (b t) -> p b t", b=GB)).then_inc(e_out[e], 16)

                for e in range(E):
                    pool.wait_ge(decay_ready, g * E + (e + 1))
                    store(2, e)
                for j, which in ((1, 1), (2, 3), (3, 0)):
                    for e in range(E):
                        evacuated(pool, hb, P_AT[j] + e)
                        store(which, e)

            steps(pool, step)

        @block.scalar
        def _(act):
            act.sem_inc(dense_free[0], 1)
            act.sem_inc(dense_free[1], 1)
            act.dma_start(colt[:, :], cols).then_inc(cols_in, 16)
            act.dma_start(Wq[:, :, :], wq.rearrange("(c p) n -> p c n", p=P)).then_inc(wq_in, 16)
            act.dma_start(cb[:, :], cproj_b.partition_broadcast(LQ)).then_inc(params_in, 16)
            act.dma_start(Wc[:, :, :], wc.rearrange("(c p) n -> p c n", p=P)).then_inc(params_in, 16)
            act.dma_start(pb[:, :], proj_b.partition_broadcast(LQ)).then_inc(params_in, 16)
            act.dma_start(mw1[:, :, :], maa_w1.rearrange("(c p) n -> p c n", p=P)).then_inc(params_in, 16)
            act.dma_start(mw2[:, :], maa_w2[0:P, :]).then_inc(params_in, 16)
            act.dma_start(mw2b[:, :], maa_w2[P:5 * DM, :]).then_inc(params_in, 16)
            act.dma_start(tw1[:, :, :], td_w1.rearrange("(c p) n -> p c n", p=P)).then_inc(params_in, 16)
            act.dma_start(tw2[:, :], td_w2).then_inc(params_in, 16)
            act.dma_start(shc[:, 0, :, :], shiftcols[:, 0, :, :]).then_inc(params_in, 16)
            act.dma_start(shc[:, 1, :, :], shiftcols[:, 1, :, :]).then_inc(params_in, 16)
            act.dma_start(ucol[:, :], u).then_inc(params_in, 16)
            act.wait_ge(cols_in, 16)

            def copy_cols(dst, psum, w, bcol, e):
                return nc.scalar.activation(dst, psum, ACT.Identity, bias=col(bcol, e), scale=col(w, e))

            def keys(hb, k, e, half_):
                ready(act, hb, k)
                nc.scalar.activation(KT[:, half_, e, :], dense[k % 2][:, 0:LK], ACT.Identity,
                                     bias=col("k_b", e)).then_inc(dense_free[k % 2], 1)

            def values(hb, k, chunk, half_):
                ready(act, hb, k)
                nc.scalar.activation(V[:, half_, chunk, :, 0:HD],
                                     dense[k % 2][0:KW, :].rearrange("p (h d) -> p h d", h=H),
                                     ACT.Copy).then_inc(dense_free[k % 2], 1)

            for e in range(E):
                keys(0, PK + e, e, 0)
            act.wait_ge(consts_made, 6)
            values(0, PV0, 0, 0)
            for k, es in ((PXA, (0, 1)), (PXB, (2, 3))):
                ready(act, 0, k)
                for e in es:
                    last_ = copy_cols(xnT[:, e, :], dense[k % 2][:, (e % 2) * LQ:(e % 2 + 1) * LQ], "ln1_w", "ln1_b", e)
                last_.then_inc(dense_free[k % 2], 1)
            values(0, PV1, 1, 0)
            values(0, PV2, 2, 0)

            def repeat_decays(gp, b, q, rkw=rkw):
                last = isinstance(gp, int)
                if not last:
                    act.wait_ge(rkw_in, channels_loaded(gp, b))
                if q >= 2 or last and b >= 1:
                    act.wait_ge(scan_step, gp * RS + b * 4 + q)
                nc.scalar.activation(wrep[:, q % 2, :].rearrange("p (j t) -> p j t", j=JH),
                                     rkw[:, q, 2, :].unsqueeze(1).to_broadcast([P, JH, LQ]),
                                     ACT.Copy).then_inc(wrep_ready, 1)

            def seq(scan):
                def body(g, b, par, n):
                    hb, nxt = half_seq(g, b), 1 - par

                    def move_pT(u):
                        act.wait_ge(pT_ready, n * H + (u + 1))
                        if u >= 2:
                            act.wait_ge(pv_ready, n * H + (u - 1))
                        nc.scalar.activation(probT[:, u % 2, :], pT[u % 2][0:KW, 0:KC * LQ],
                                             ACT.Copy).then_inc(probT_ready, 1)

                    for u in range(H):
                        act.wait_ge(sm_ready, n * H + (u + 1))
                        if u >= 2:
                            act.wait_ge(pT_ready, n * H + (u - 1))
                        nc.scalar.activation(prob[:, u % 2, :], sm[:, u % 2, :], ACT.Exp,
                                             bias=nm[:, u % 2:u % 2 + 1], scale=-1.0).then_inc(prob_ready, 1)
                        if u >= 1:
                            move_pT(u - 1)
                        if scan and u in (0, 3, 7, 11):
                            repeat_decays(g - 1, b, (u + 1) // 4)
                        if u in (1, 3, 5, 7):
                            keys(hb, TK + u // 2, u // 2, nxt)
                        elif u == 9:
                            values(hb, TV0, 0, nxt)
                        elif u == 10:
                            ready(act, hb, TX)
                            for e in range(E):
                                last_ = copy_cols(xnT[:, e, :], dense[TX % 2][:, e * LQ:(e + 1) * LQ],
                                                  "ln1_w", "ln1_b", e)
                            last_.then_inc(dense_free[TX % 2], 1)
                    move_pT(H - 1)
                    values(hb, TV1, 1, nxt)
                    values(hb, TV2, 2, nxt)
                    ready(act, hb, TY)
                    for e in range(E):
                        last_ = copy_cols(YT[:, e, bass.ds(b * LQ, LQ)], dense[TY % 2][:, e * LQ:(e + 1) * LQ],
                                          "ln2_w", "ln2_b", e)
                    last_.then_inc(dense_free[TY % 2], 1)
                return body

            def ln_cols(hb, first_tile, w, bcol):
                for b in range(GB):
                    k = first_tile + b
                    ready(act, hb, k)
                    for e in range(E):
                        last_ = copy_cols(XA[:, e, b, 1:LQ + 1], dense[k % 2][:, e * LQ:(e + 1) * LQ], w, bcol, e)
                    last_.then_inc(dense_free[k % 2], 1)

            def group_std(gp):
                act.wait_ge(var_ready["gn"], gp + 1)
                nc.scalar.activation(gst[:, 2, :], gst[:, 1, :], ACT.Sqrt, bias=eps_col[:, :],
                                     scale=1.0 / RS).then_inc(rstd_ready["gn"], 1)

            def mlp(g):
                hb = half_mlp(g)
                for m in range(4):
                    if m == 1 and not (isinstance(g, int) and g == 0):
                        group_std(g - 1)
                    if m >= 1:
                        act.wait_ge(mlp_used, g * 3 + m)
                    for e in range(E):
                        k = 4 * m + e
                        ready(act, hb, k)
                        nc.scalar.activation(HT[:, e, :], dense[k % 2][:, 0:T], ACT.Gelu_apprx_tanh,
                                             bias=colt[:, FCB + k:FCB + k + 1]).then_inc(dense_free[k % 2], 1)

            def post(g):
                hb = half_post(g)
                ln_cols(hb, O_LN, "r_ln2_w", "r_ln2_b")
                for e in range(E):
                    k = O_FK + e
                    ready(act, hb, k)
                    nc.scalar.activation(HT[:, e, :], dense[k % 2][:, 0:T], ACT.Relu).then_inc(dense_free[k % 2], 1)
                for e in range(E):
                    evacuated(act, hb, O_FK + e)
                    nc.scalar.activation(HT[:, e, :], HT[:, e, :], ACT.Square).then_inc(kk_ready, 1)
                if not (isinstance(g, int) and g == NG):
                    ln_cols(*ln_tiles(g), "r_ln1_w", "r_ln1_b")
                for b in range(GB):
                    k = frv_at(g) + 2 * b
                    ready(act, hb, k)
                    if b >= 2:
                        act.wait_ge(out_ready, (g - 1) * GB + (b - 1))
                    nc.scalar.activation(RR[b % 2], dense[k % 2][0:LQ, :], ACT.Sigmoid).then_inc(dense_free[k % 2], 1)

            def pre(g):
                hb = half_pre(g)
                if isinstance(g, int) and g == 0:
                    ln_cols(*ln_tiles(g), "r_ln1_w", "r_ln1_b")
                ready(act, hb, R_W1)
                nc.scalar.activation(TA[:, :], dense[R_W1 % 2][:, 0:T], ACT.Tanh)
                nc.scalar.activation(TB[:, :], score[0][0:DM, 0:T], ACT.Tanh).then_inc(dense_free[R_W1 % 2], 1)
                ready(act, hb, TD1)
                nc.scalar.activation(TD, dense[TD1 % 2][0:DD, 0:T], ACT.Tanh).then_inc(dense_free[TD1 % 2], 1)
                for e in range(E):
                    k = TD2 + e
                    ready(act, hb, k)
                    nc.scalar.activation(HT[:, e, :], dense[k % 2][:, 0:T], ACT.Exp,
                                         bias=col("decay", e)).then_inc(dense_free[k % 2], 1)
                for e in range(E):
                    evacuated(act, hb, TD2 + e)
                    nc.scalar.activation(HT[:, e, :], HT[:, e, :], ACT.Exp, scale=-1.0).then_inc(decay_ready, 1)
                for j in (1, 2, 3):
                    for e in range(E):
                        k = P_AT[j] + e
                        ready(act, hb, k)
                        act.wait_ge(e_out[e], g * 64 + 16 * j)
                        nc.scalar.activation(HT[:, e, :], dense[k % 2][:, 0:T],
                                             ACT.Copy).then_inc(dense_free[k % 2], 1)
                for e in range(E):
                    k = P_AT[4] + e
                    ready(act, hb, k)
                    nc.scalar.activation(GT[:, e, :], dense[k % 2][:, 0:T], ACT.Silu).then_inc(dense_free[k % 2], 1)

            def step(g):
                first, last = isinstance(g, int) and g == 0, isinstance(g, int) and g == NG
                if last:
                    act.wait_ge(consts_made, 9)
                    for b in range(GB):
                        for q in range(4):
                            if q == 0:
                                last_loaded(act, b)
                            repeat_decays(g - 1, b, q, rkw_last[b])
                    group_std(g - 1)
                else:
                    sequences(act, g, seq(not first))
                    mlp(g)
                if not first:
                    post(g)
                if not last:
                    pre(g)

            steps(act, step)

        @block.vector
        def _(dve):
            scan = Chain(dve, scan_chain)
            gn = Chain(dve, gn_chain)

            def row_stats(p, src, count, slot=0):
                if count is not None:
                    dve.wait_ge(xn_ready[p], count - 1)
                apart(dve)
                nc.vector.bn_stats(bst[p][:, slot, :], src).then_inc(stats_ready[p], 1)

            def row_var(p, count, slot=0):
                dve.wait_ge(stats_ready[p], count)
                apart(dve)
                nc.vector.bn_aggr(mv[p][:, slot, :], bst[p][:, slot, :]).then_inc(var_ready[p], 1)

            def row_apply(p, src, par, count, slot=0):
                dve.wait_ge(rstd_ready[p], count)
                nc.vector.tensor_scalar(xn[:, par, :], src, mv[p][:, slot, 0:1], rstd[p][:, slot:slot + 1],
                                        ALU.subtract, ALU.mult).then_inc(xn_ready[p], 1)

            def query(hb, k, half_):
                ready(dve, hb, k)
                nc.vector.tensor_tensor(qT[:, half_, :, :], dense[k % 2][:, 0:T].rearrange("p (e t) -> p e t", e=E),
                                        colb("q_b", LQ), ALU.add).then_inc(dense_free[k % 2], 1)

            dve.sem_inc(scan_step, 1)
            dve.wait_ge(x_in, 16)
            row_stats("seq", x_t[:, :], None)
            row_var("seq", 1)
            row_apply("seq", x_t[:, :], 0, 1)
            dve.wait_ge(cols_in, 16)
            query(0, PQ, 0)
            dve.wait_ge(params_in, 16 * PARAMS)

            def recurrence(gp, b, q, stage):
                i = b * 4 + q
                r, kk = rkw[:, q, 0, :], rkw[:, q, 1, :]
                if stage == 0:
                    scan.start((gp * RS + i) * CHANNEL)
                    if q == 0:
                        dve.wait_ge(rkw_in, channels_loaded(gp, b))
                    dve.wait_ge(scan_step, gp * RS + (i + 1))
                    scan.step(nc.vector.scalar_tensor_tensor(out=bon[:, 1, :], in0=r, scalar=ucol[:, bass.ds(i, 1)],
                                                             in1=kk, op0=ALU.mult, op1=ALU.mult))
                    scan.step(nc.vector.tensor_tensor(S[:, :, 1:LQ], VB[:, :, 0:LQ - 1],
                                                      kk[:, 0:LQ - 1].unsqueeze(1).to_broadcast([P, RS, LQ - 1]),
                                                      ALU.mult))
                    scan.step(nc.vector.tensor_copy(S[:, :, 0], s0[:, bass.ds(i, 1), :].rearrange("p a j -> p (a j)")))
                elif stage == 1:
                    scan.settle()
                    scan.step(nc.vector.tensor_tensor(bon[:, 0, :], bon[:, 0, :], bon[:, 1, :], ALU.add))
                    dve.wait_ge(wrep_ready, gp * RS + (i + 1))
                    for jh in range(RS // JH):
                        part = S[:, jh * JH:(jh + 1) * JH, :].rearrange("p j t -> p (j t)")
                        scan.step(nc.vector.tensor_tensor_scan(out=part, data0=wrep[:, q % 2, :], data1=part,
                                                               initial=0.0, op0=ALU.mult, op1=ALU.add))
                elif stage == 2:
                    scan.settle()
                    scan.step(nc.vector.tensor_tensor(S[:, :, :], S[:, :, :],
                                                      r.unsqueeze(1).to_broadcast([P, RS, LQ]), ALU.mult))
                else:
                    scan.settle()
                    nc.vector.tensor_tensor(YB[:, :, :], YB[:, :, :], S[:, :, :], ALU.add).then_inc(scan_step, 1)
                    scan.end(CHANNEL)

            def recurrence_last(gp):
                scan.start(gp * RS * CHANNEL)
                for i in range(RS):
                    b, q = i // 4, i % 4
                    r, rk, St = rkw_last[b][:, q, 0, :], rkw_last[b][:, q, 1, :], S_last[q]
                    if q == 0:
                        last_loaded(dve, b)
                    dve.wait_ge(kv_ready, 2 * i + 2)
                    scan.step(nc.vector.tensor_copy(St[:, :, 0], s0[:, i, :]))
                    scan.step(nc.vector.scalar_tensor_tensor(out=bon[:, 0, :], in0=rk, scalar=ucol[:, i:i + 1],
                                                             in1=bon[:, 0, :], op0=ALU.mult, op1=ALU.add))
                    scan.settle()
                    dve.wait_ge(wrep_ready, gp * RS + (i + 1))
                    for jh in range(RS // JH):
                        part = St[:, jh * JH:(jh + 1) * JH, :].rearrange("p j t -> p (j t)")
                        scan.step(nc.vector.tensor_tensor_scan(out=part, data0=wrep[:, q % 2, :], data1=part,
                                                               initial=0.0, op0=ALU.mult, op1=ALU.add))
                    scan.settle()
                    nc.vector.tensor_tensor(St[:, :, :], St[:, :, :], r.unsqueeze(1).to_broadcast([P, RS, LQ]),
                                            ALU.mult).then_inc(scan_step, 1)

            def seq(with_scan):
                def body(g, b, par, n):
                    hb, nxt = half_seq(g, b), 1 - par

                    def normalise(k):
                        dve.wait_ge(pv_ready, n * H + 8 * (k + 1))
                        o = obank[k][0:LQ, 0:8 * (HD + 1)].rearrange("p (h d) -> p h d", h=8)
                        nc.vector.reciprocal(rden[:, 8 * k:8 * k + 8], o[:, :, HD]).then_inc(den_ready, 1)
                        dve.wait_ge(den_ready, n * 2 + (k + 1))
                        nc.vector.tensor_tensor(on[:, 256 * k:256 * (k + 1)].rearrange("p (h d) -> p h d", h=8),
                                                o[:, :, 0:HD],
                                                rden[:, 8 * k:8 * k + 8].unsqueeze(2).to_broadcast([LQ, 8, HD]),
                                                ALU.mult).then_inc(on_ready, 1)

                    dve.wait_ge(maskb_ready, n + 1)
                    for u in range(H):
                        dve.wait_ge(score_ready, n * H + (u + 1))
                        if u >= 2:
                            dve.wait_ge(prob_ready, n * H + (u - 1))
                        apart(dve)
                        nc.vector.tensor_tensor_reduce(
                            out=sm[:, u % 2, :], in0=score[u % 2][0:LQ, 0:LK], in1=maskb[:, :], scale=-SCALE,
                            scalar=3.0e38, op0=ALU.add, op1=ALU.min,
                            accum_out=nm[:, u % 2:u % 2 + 1]).then_inc(sm_ready, 1)
                        if u == 6:
                            dve.wait_ge(x_in, n * 16 + 32)
                            row_stats("seq", x_t[:, :], n * 2 + 2)
                            row_var("seq", n * 2 + 2)
                        elif u == 8:
                            row_apply("seq", x_t[:, :], 0, n * 2 + 2)
                        elif u == 10:
                            normalise(0)
                        elif u == 14:
                            query(hb, TQ, nxt)
                        if with_scan:
                            recurrence(g - 1, b, u // 4, u % 4)
                    normalise(1)
                    ready(dve, hb, TO)
                    nc.vector.tensor_tensor(onT[:, :, :], dense[TO % 2][:, 0:T].rearrange("p (e t) -> p e t", e=E),
                                            colb("v_b", LQ), ALU.add).then_inc(dense_free[TO % 2], 1)
                    ready(dve, hb, TC)
                    dve.wait_ge(res_ready, n + 1)
                    rows = X[:, (g % 2) * GB + b, :]
                    nc.vector.tensor_tensor(rows, dense[TC % 2][0:LQ, :], res[:, :], ALU.add
                                            ).then_inc(dense_free[TC % 2], 1)
                    evacuated(dve, hb, TC)
                    row_stats("seq", rows, n * 2 + 3)
                    row_var("seq", n * 2 + 3)
                    row_apply("seq", rows, 1, n * 2 + 3)
                return body

            def over_j(v):
                return v.unsqueeze(1).to_broadcast([P, RS, LQ])

            def group_norm(gp):
                GN = 8
                last = isinstance(gp, int)
                gn.start(gp * GN)
                dve.wait_ge(scan_step, gp * RS + (RS + 1))
                gn.step(nc.vector.tensor_tensor(VB[:, :, :], VB[:, :, :], over_j(bon[:, 0, :]), ALU.mult))
                gn.settle()
                if last:
                    dve.wait_ge(summed, RS)
                    for k in range(E):
                        part = slice(GB * k, GB * (k + 1))
                        last_ = nc.vector.tensor_tensor(
                            YB[:, part, :], acc[k][:, 0:T].rearrange("p (j t) -> p j t", j=GB), VB[:, part, :], ALU.add)
                    gn.step(last_)
                else:
                    gn.step(nc.vector.tensor_tensor(YB[:, :, :], YB[:, :, :], VB[:, :, :], ALU.add))
                gn.settle()
                gn.step(nc.vector.tensor_reduce(gst[:, 0, :], YB[:, :, :].rearrange("p j t -> p t j"),
                                                axis=AX.X, op=ALU.add))
                gn.settle()
                gn.step(nc.vector.tensor_scalar(gst[:, 0, :], gst[:, 0, :], 1.0 / RS, None, ALU.mult))
                gn.settle()
                gn.step(nc.vector.tensor_tensor(YB[:, :, :], YB[:, :, :], over_j(gst[:, 0, :]), ALU.subtract))
                gn.settle()
                gn.step(nc.vector.tensor_tensor(VB[:, :, :], YB[:, :, :], YB[:, :, :], ALU.mult))
                gn.settle()
                nc.vector.tensor_reduce(gst[:, 1, :], VB[:, :, :].rearrange("p j t -> p t j"),
                                        axis=AX.X, op=ALU.add).then_inc(var_ready["gn"], 1)
                dve.wait_ge(rstd_ready["gn"], gp + 1)
                gn.step(nc.vector.reciprocal(gst[:, 2, :], gst[:, 2, :]))
                gn.settle()
                nc.vector.tensor_tensor(YB[:, :, :], YB[:, :, :], over_j(gst[:, 2, :]), ALU.mult).then_inc(y_norm, 1)
                gn.step(nc.vector.memset(bon[:, 0, :], 0.0))
                gn.end(GN)

            def shift_and_mix(p, which, gp, dst, name, done):
                def shift(e):
                    dve.wait_ge(shift_ready[p], gp * 5 + 1)
                    nc.vector.tensor_tensor(SX[:, GB * e:GB * (e + 1), :], XAc[:, GB * e:GB * (e + 1), 0:LQ],
                                            XAc[:, GB * e:GB * (e + 1), 1:LQ + 1],
                                            ALU.subtract).then_inc(shift_ready[p], 1)

                nc.vector.tensor_copy(XA[:, :, :, 0], shc[:, which, :, bass.ds(gp * GB, GB)]).then_inc(shift_ready[p], 1)
                shift(0)
                for e in range(E):
                    if e + 1 < E:
                        shift(e + 1)
                    dve.wait_ge(shift_ready[p], gp * 5 + (e + 2))
                    mix_block(dst, name, e).then_inc(done, 1)

            def mix_block(dst, name, e):
                return nc.vector.scalar_tensor_tensor(
                    out=dst[:, e, :].rearrange("p (b t) -> p b t", b=GB), in0=SX[:, GB * e:GB * (e + 1), :],
                    scalar=col(name, e), in1=XAs[:, e, :, :], op0=ALU.mult, op1=ALU.add)

            def gate(g):
                dve.wait_ge(y_in, g * 64)
                for e in range(E):
                    last_ = nc.vector.tensor_scalar(C[0][:, e, :], C[0][:, e, :], col("gn_w", e), col("gn_b", e),
                                                    ALU.mult, ALU.add)
                last_.then_inc(gn_scaled, 1)
                dve.wait_ge(gn_scaled, g)
                nc.vector.tensor_tensor(C[0][:, :, :], C[0][:, :, :], GT[:, :, :], ALU.mult).then_inc(og_ready, 1)

            def mlp_bias(g):
                at = (g % 2) * GB
                rows = X[:, at:at + GB, :] if isinstance(g, int) else X[:, bass.ds(at, GB), :]
                dve.wait_ge(xn_ready["seq"], g * 8 + 9)
                nc.vector.tensor_tensor(rows, rows, pb[:, :].unsqueeze(1).to_broadcast([LQ, GB, D]),
                                        ALU.add).then_inc(bias_added, 1)
                dve.wait_ge(bias_added, g + 1)

            def mlp_add(g):
                for b in range(GB):
                    rows = X[:, (g % 2) * GB + b, :]
                    dve.wait_ge(acc_ready, g * GB + (b + 1))
                    nc.vector.tensor_tensor(rows, rows, acc[b][0:LQ, :], ALU.add).then_inc(x1_ready, 1)

            def rows_of(g, b):
                return X[:, (g % 2) * GB + b, :]

            def pre_stats(g, b):
                dve.wait_ge(x1_ready, g * GB + (b + 1))
                row_stats("pre", rows_of(g, b), None, b)
                row_var("pre", g * GB + (b + 1), b)

            def pre_rows(g):
                for b in range(GB):
                    if b >= 2:
                        ready(dve, ln_tiles(g)[0], ln_tiles(g)[1] + b - 2)
                    row_apply("pre", rows_of(g, b), b % 2, g * GB + (b + 1), b)
                evacuated(dve, ln_tiles(g)[0], ln_tiles(g)[1] + 2)
                evacuated(dve, ln_tiles(g)[0], ln_tiles(g)[1] + 3)
                shift_and_mix("pre", 1, g, C[0], "maa_x", mix_ready)

            def post(g):
                hb = half_post(g)
                last = isinstance(g, int) and g == NG
                for b in range(GB):
                    k = O_OUT + b
                    count = (g - 1) * GB + (b + 1)
                    rows = rows_of(g - 1, b)
                    ready(dve, hb, k)
                    nc.vector.tensor_tensor(rows, rows, dense[k % 2][0:LQ, :],
                                            ALU.add).then_inc(dense_free[k % 2], 1)
                    evacuated(dve, hb, k)
                    row_stats("post", rows, None, b)
                    row_var("post", count, b)
                    if not last:
                        pre_stats(g, b)
                    if b >= 2:
                        ready(dve, hb, O_LN + b - 2)
                    row_apply("post", rows, b % 2, count, b)
                evacuated(dve, hb, O_LN + 2)
                evacuated(dve, hb, O_LN + 3)
                shift_and_mix("post", 0, g - 1, C[0], "mix_k", ck_ready)
                for e in range(E):
                    last_ = mix_block(C[1], "mix_r", e)
                last_.then_inc(ck_ready, 1)
                if not last:
                    pre_rows(g)
                for b in range(GB):
                    k = frv_at(g) + 2 * b + 1
                    rows = rows_of(g - 1, b)
                    evacuated(dve, hb, k - 1)
                    ready(dve, hb, k)
                    nc.vector.tensor_tensor(RR[b % 2], dense[k % 2][0:LQ, :], RR[b % 2],
                                            ALU.mult).then_inc(dense_free[k % 2], 1)
                    evacuated(dve, hb, k)
                    nc.vector.tensor_tensor(rows, rows, RR[b % 2], ALU.add).then_inc(out_ready, 1)

            def pre(g):
                hb = half_pre(g)
                if isinstance(g, int) and g == 0:
                    for b in range(GB):
                        pre_stats(g, b)
                    pre_rows(g)
                for j in range(5):
                    dst = C[j % 2]
                    for e in range(E):
                        k = X_AT[j] + e
                        ready(dve, hb, k)
                        nc.vector.scalar_tensor_tensor(
                            out=dst[:, e, :], in0=dense[k % 2][:, 0:T], scalar=col(f"maa_{ORDER[j]}", e),
                            in1=SX[:, GB * e:GB * (e + 1), :].rearrange("p b t -> p (b t)"),
                            op0=ALU.add, op1=ALU.mult).then_inc(dense_free[k % 2], 1)
                    for e in range(E):
                        evacuated(dve, hb, X_AT[j] + e)
                        last_ = nc.vector.tensor_tensor(dst[:, e, :].rearrange("p (b t) -> p b t", b=GB),
                                                        dst[:, e, :].rearrange("p (b t) -> p b t", b=GB),
                                                        XAs[:, e, :, :], ALU.add)
                    last_.then_inc(mix_ready, 1)
                if not (isinstance(g, int) and g == 0):
                    dve.wait_ge(out_done, g * 64)
                    apart(dve)
                nc.vector.memset(YB[:, :, :], 0.0).then_inc(yb_zero, 1)
                dve.wait_ge(yb_zero, g + 1)
                apart(dve)

            nc.vector.memset(bon[:, 0, :], 0.0).then_inc(bon_zero, 1)
            dve.wait_ge(bon_zero, 1)

            def step(g):
                first, last = isinstance(g, int) and g == 0, isinstance(g, int) and g == NG
                if not first:
                    dve.wait_ge(v_in, g * 80)
                    apart(dve)
                if not last:
                    sequences(dve, g, seq(not first))
                else:
                    recurrence_last(g - 1)
                if not first:
                    group_norm(g - 1)
                if not last:
                    mlp_bias(g)
                if not first:
                    gate(g)
                if not last:
                    mlp_add(g)
                if not first:
                    post(g)
                if not last:
                    pre(g)

            steps(dve, step)

        @block.tensor
        def _(pe):
            pe.sem_inc(dense_ready, READY0)
            for k in range(SLOTS):
                pe.sem_inc(ring_used[k], 1)

            def product(out_ap, pairs, lo=0, hi=None):
                hi = len(pairs) if hi is None else hi
                for k in range(lo, hi):
                    last_ = nc.tensor.matmul(out_ap, pairs[k][0], pairs[k][1], start=(k == 0),
                                             stop=(k == len(pairs) - 1))
                return last_

            def part(hb, k, out_ap, pairs, piece):
                if piece != 1:
                    bank_free(pe, hb, k)
                mid = len(pairs) // 2
                last_ = product(out_ap, pairs, mid if piece == 1 else 0, mid if piece == 0 else None)
                if piece != 0:
                    last_.then_inc(dense_ready, 1)

            def keys(hb, k, e, piece=None):
                part(hb, k, dense[k % 2][:, 0:LK],
                     [(Wk[:, c, e * P:(e + 1) * P], ctx_t[:, c, :]) for c in range(E)], piece)

            def values(hb, k, chunk, piece=None):
                part(hb, k, dense[k % 2][0:KW, :],
                     [(ctx_t[:, c, chunk * KW:(chunk + 1) * KW], Wv[:, c, :]) for c in range(E)], piece)

            def rows_to_cols(k, rows, es=range(E)):
                for at, e in enumerate(es):
                    last_ = nc.tensor.transpose(dense[k % 2][:, at * LQ:(at + 1) * LQ], rows[:, e * P:(e + 1) * P],
                                                ident[0:LQ, 0:LQ])
                last_.then_inc(dense_ready, 1)

            def query(k, es=range(E)):
                for e in es:
                    last_ = product(dense[k % 2][:, e * LQ:(e + 1) * LQ],
                                    [(Wq[:, c, e * P:(e + 1) * P], xnT[:, c, :]) for c in range(E)])
                if E - 1 in es:
                    last_.then_inc(dense_ready, 1)

            pe.wait_ge(ctx_in, 16)
            pe.wait_ge(wk_in, 16)
            for e in range(E):
                keys(0, PK + e, e)
            pe.wait_ge(wv_in, 16)
            values(0, PV0, 0)
            pe.wait_ge(consts_made, 6)
            pe.wait_ge(xn_ready["seq"], 1)
            for k, es in ((PXA, (0, 1)), (PXB, (2, 3))):
                bank_free(pe, 0, k)
                rows_to_cols(k, xn[:, 0, :], es)
            evacuated(pe, 0, PXA)
            evacuated(pe, 0, PXB)
            pe.wait_ge(wq_in, 16)
            query(PQ)
            values(0, PV1, 1)
            values(0, PV2, 2)
            pe.wait_ge(params_in, 16 * PARAMS)
            evacuated(pe, 0, PQ)
            evacuated(pe, 0, PV1)
            evacuated(pe, 0, PV2)

            def seq(g, b, par, n):
                hb = half_seq(g, b)

                def scores(u):
                    if u >= 2:
                        pe.wait_ge(sm_ready, n * H + (u - 1))
                    r = HD * (u % 4)
                    nc.tensor.matmul(score[u % 2][0:LQ, 0:LK], qT[r:r + HD, par, u // 4, :],
                                     KT[r:r + HD, par, u // 4, :], start=True, stop=True).then_inc(score_ready, 1)

                def turn(u):
                    pe.wait_ge(prob_ready, n * H + (u + 1))
                    if u >= 2:
                        pe.wait_ge(probT_ready, n * H + (u - 1))
                    for k in range(KC):
                        last_ = nc.tensor.transpose(pT[u % 2][0:KW, k * LQ:(k + 1) * LQ],
                                                    prob[:, u % 2, k * KW:(k + 1) * KW], ident[0:LQ, 0:LQ])
                    last_.then_inc(pT_ready, 1)

                def weigh(u):
                    pe.wait_ge(probT_ready, n * H + (u + 1))
                    at = (u % 8) * (HD + 1)
                    product(obank[u // 8][0:LQ, at:at + HD + 1],
                            [(probT[:, u % 2, k * LQ:(k + 1) * LQ], V[:, par, k, u, :]) for k in range(KC)]
                            ).then_inc(pv_ready, 1)

                scores(0)
                scores(1)
                for u in range(H):
                    if u + 2 < H:
                        scores(u + 2)
                    if u == 0:
                        pe.wait_ge(ctx_in, n * 16 + 32)
                    if u < 8:
                        keys(hb, TK + u // 2, u // 2, u % 2)
                    elif u in (8, 9):
                        values(hb, TV0, 0, u % 2)
                    elif u == 10:
                        pe.wait_ge(xn_ready["seq"], n * 2 + 2)
                        bank_free(pe, hb, TX)
                        rows_to_cols(TX, xn[:, 0, :])
                    elif u == 12:
                        evacuated(pe, hb, TX)
                        bank_free(pe, hb, TQ)
                        query(TQ, (0, 1))
                    elif u == 13:
                        query(TQ, (2, 3))
                    elif u == 15:
                        values(hb, TV1, 1, 0)
                    turn(u)
                    if u >= 1:
                        weigh(u - 1)
                weigh(H - 1)
                values(hb, TV1, 1, 1)
                pe.wait_ge(on_ready, n * 2 + 2)
                bank_free(pe, hb, TO)
                rows_to_cols(TO, on)
                evacuated(pe, hb, TO)
                bank_free(pe, hb, TC)
                product(dense[TC % 2][0:LQ, :], [(onT[:, c, :], Wc[:, c, :]) for c in range(E)]
                        ).then_inc(dense_ready, 1)
                values(hb, TV2, 2)
                pe.wait_ge(xn_ready["seq"], n * 2 + 3)
                bank_free(pe, hb, TY)
                rows_to_cols(TY, xn[:, 1, :])
                evacuated(pe, hb, TV1)
                evacuated(pe, hb, TV2)

            def weights(g, k):
                pe.wait_ge(ring_in[k % SLOTS], (half_piece(g) + (k // SLOTS + 1)) * 16)
                return ring[:, k % SLOTS, :, :]

            def channels_out(hb, first_tile, w, src, blocks=None, base=0):
                for e in range(E):
                    k = first_tile + e
                    bank_free(pe, hb, k)
                    pairs = [(w[:, c, e * P:(e + 1) * P], src[:, c, :]) for c in range(E)]
                    for c in range(E):
                        if e == 0 and blocks is not None:
                            pe.wait_ge(blocks, base + (c + 1))
                        last_ = product(dense[k % 2][:, 0:T], pairs, c, c + 1)
                    last_.then_inc(dense_ready, 1)

            def ln_rows(g):
                for b in range(GB):
                    pe.wait_ge(xn_ready["pre"], g * GB + (b + 1))
                    bank_free(pe, ln_tiles(g)[0], ln_tiles(g)[1] + b)
                    rows_to_cols(R_LN + b, xn[:, b % 2, :])

            def used(k, hb, tile):
                ready(pe, hb, tile)
                pe.sem_inc(ring_used[k % SLOTS], 1)

            def mlp(g):
                hb = half_mlp(g)
                bank_free(pe, hb, 1)
                for m in range(4):
                    w = weights(g, 2 * m)
                    channels_out(hb, 4 * m, w, YT)
                    used(2 * m, hb, 4 * m + 3)
                    w = weights(g, 2 * m + 1)
                    evacuated(pe, hb, 4 * m + 2)
                    evacuated(pe, hb, 4 * m + 3)
                    for b in range(GB):
                        for c in range(E):
                            last_ = nc.tensor.matmul(acc[b][0:LQ, :], HT[:, c, b * LQ:(b + 1) * LQ], w[:, c, :],
                                                     start=(m == 0 and c == 0), stop=(m == 3 and c == E - 1))
                        if m == 3:
                            last_.then_inc(acc_ready, 1)
                    if m < 3:
                        last_.then_inc(mlp_used, 1)
                        pe.wait_ge(mlp_used, g * 3 + (m + 1))
                    else:
                        pe.wait_ge(acc_ready, g * GB + GB)
                    pe.sem_inc(ring_used[1], 1)

            def post(g):
                hb, gp = half_post(g), g - 1
                last = isinstance(g, int) and g == NG
                first_w, frv = 0 if last else 8, frv_at(g)
                w = weights(g, first_w)
                pe.wait_ge(og_ready, g)
                for b in range(GB):
                    k = O_OUT + b
                    bank_free(pe, hb, k)
                    product(dense[k % 2][0:LQ, :], [(C[0][:, c, b * LQ:(b + 1) * LQ], w[:, c, :]) for c in range(E)]
                            ).then_inc(dense_ready, 1)
                used(first_w, hb, O_OUT + 3)
                for b in range(GB):
                    pe.wait_ge(xn_ready["post"], gp * GB + (b + 1))
                    bank_free(pe, hb, O_LN + b)
                    rows_to_cols(O_LN + b, xn[:, b % 2, :])
                w = weights(g, first_w + 1)
                channels_out(hb, O_FK, w, C[0], ck_ready, gp * 5)
                used(first_w + 1, hb, O_FK + 3)
                if not last:
                    ln_rows(g)
                wr = weights(g, first_w + 2)
                wfv = weights(g, first_w + 3)
                pe.wait_ge(ck_ready, gp * 5 + 5)
                for b in range(GB):
                    k = frv + 2 * b
                    bank_free(pe, hb, k)
                    product(dense[k % 2][0:LQ, :], [(C[1][:, c, b * LQ:(b + 1) * LQ], wr[:, c, :]) for c in range(E)]
                            ).then_inc(dense_ready, 1)
                    if b == 0:
                        pe.wait_ge(kk_ready, gp * E + E)
                    bank_free(pe, hb, k + 1)
                    product(dense[(k + 1) % 2][0:LQ, :],
                            [(HT[:, c, b * LQ:(b + 1) * LQ], wfv[:, c, :]) for c in range(E)]
                            ).then_inc(dense_ready, 1)
                used(first_w + 2, hb, frv + 7)
                used(first_w + 3, hb, frv + 7)

            def pre(g):
                hb = half_pre(g)
                first_w = 8 if isinstance(g, int) and g == 0 else 12
                if isinstance(g, int) and g == 0:
                    ln_rows(g)
                bank_free(pe, hb, R_W1)
                for c in range(E):
                    pe.wait_ge(mix_ready, g * 9 + (c + 1))
                    product(dense[R_W1 % 2][:, 0:T], [(mw1[:, c_, 0:P], C[0][:, c_, :]) for c_ in range(E)], c, c + 1)
                product(score[0][0:DM, 0:T], [(mw1[:, c, P:5 * DM], C[0][:, c, :]) for c in range(E)]
                        ).then_inc(dense_ready, 1)

                def low_rank(j):
                    q = ORDER[j]
                    w, a = (mw2b, TB[:, :]) if q == 4 else (mw2[DM * q:DM * (q + 1), :], TA[DM * q:DM * (q + 1), :])
                    for e in range(E):
                        k = X_AT[j] + e
                        bank_free(pe, hb, k)
                        nc.tensor.matmul(dense[k % 2][:, 0:T], w[:, e * P:(e + 1) * P], a,
                                         start=True, stop=True).then_inc(dense_ready, 1)

                evacuated(pe, hb, R_W1)
                low_rank(0)
                low_rank(1)
                pe.wait_ge(mix_ready, g * 9 + 5)
                bank_free(pe, hb, TD1)
                product(dense[TD1 % 2][0:DD, 0:T], [(tw1[:, c, :], C[0][:, c, :]) for c in range(E)]
                        ).then_inc(dense_ready, 1)
                evacuated(pe, hb, TD1)
                for e in range(E):
                    k = TD2 + e
                    bank_free(pe, hb, k)
                    nc.tensor.matmul(dense[k % 2][:, 0:T], tw2[:, e * P:(e + 1) * P], TD,
                                     start=True, stop=True).then_inc(dense_ready, 1)
                for j in range(2, 6):
                    if j < 5:
                        low_rank(j)
                    w = weights(g, first_w + j - 2)
                    pe.wait_ge(mix_ready, g * 9 + (j + 4))
                    channels_out(hb, P_AT[j - 1], w, C[(j - 1) % 2])
                    used(first_w + j - 2, hb, P_AT[j - 1] + 3)

            def step(g):
                first, last = isinstance(g, int) and g == 0, isinstance(g, int) and g == NG
                if not last:
                    sequences(pe, g, seq)
                    mlp(g)
                else:
                    for i in range(RS):
                        pe.wait_ge(scan_step, (g - 1) * RS + i + 2)
                        for k in range(E):
                            last_ = nc.tensor.matmul(
                                acc[k][:, 0:T], ident[:, :],
                                S_last[i % 4][:, GB * k:GB * (k + 1), :].rearrange("p j t -> p (j t)"),
                                start=(i == 0), stop=(i == RS - 1))
                        last_.then_inc(summed, 1)
                if not first:
                    post(g)
                if not last:
                    pre(g)

            steps(pe, step)


def kernel(x, ctx_2048, mask_BxS2_bf1, **p):
    import concourse.bacc as bacc
    from concourse.bass_utils import run_bass_kernel_spmd

    a = {k: np.asarray(v) for k, v in p.items()}
    x, ctx, mask = np.asarray(x), np.asarray(ctx_2048), np.asarray(mask_BxS2_bf1)
    l0 = {k[len("L0_xattn_"):]: v for k, v in a.items() if k.startswith("L0_xattn_")}
    l1 = {k[len("L1_xattn_"):]: v for k, v in a.items() if k.startswith("L1_xattn_")}
    vecs = [l0["ln1_w"], l0["ln1_b"], l0["q_b"], l0["k_b"], l0["v_b"], l0["ln2_w"], l0["ln2_b"],
            l1["ln1_w"], l1["ln1_b"], l1["ln2_w"], l1["ln2_b"], l1["maa_x"],
            *[l1["maa_stack"][0, j] for j in range(5)], l1["time_decay"], l1["gn_w"], l1["gn_b"],
            l1["ffn_maa_k"], l1["ffn_maa_r"], l0["fc_b"]]
    cols = np.concatenate([v.reshape(-1, P).T for v in vecs], axis=1)
    pieces = []
    for m in range(4):
        pieces += [l0["fc_w"][:, m * D:(m + 1) * D], l0["proj_w"][m * D:(m + 1) * D, :]]
    pieces += [l1[w].T for w in ("Wk", "Wv", "Wr", "Wg", "Wo", "Wfk", "Wfr", "Wfv")]
    arrays = {
        "x": x,
        "ctxT": ctx.transpose(0, 2, 1),
        "ctx": ctx,
        "mask": mask.view(np.uint8),
        "shiftcols": ctx[:, 0:2, :].reshape(B, 2, E, P).transpose(3, 1, 2, 0),
        "cols": cols,
        "wq": l0["q_w"], "wk": l0["k_w"], "wv": l0["v_w"], "wc": l0["cproj_w"],
        "cproj_b": l0["cproj_b"], "proj_b": l0["proj_b"],
        "stream": np.stack(pieces),
        "maa_w1": l1["maa_w1"], "maa_w2": l1["maa_w2"].reshape(5 * DM, D),
        "td_w1": l1["td_w1"], "td_w2": l1["td_w2"],
        "u": np.tile(l1["u"].reshape(RH, RS), (GB, 1)),
    }
    arrays = {f"in_{k}": np.ascontiguousarray(v) for k, v in arrays.items()}
    nc = bacc.Bacc("TRN2", target_bir_lowering=False, num_devices=1)
    args = [nc.dram_tensor(k, v.shape, mybir.dt.from_np(v.dtype), kind="ExternalInput").ap()
            for k, v in arrays.items()]
    out = nc.dram_tensor("out", (B, LQ, D), F32, kind="ExternalOutput").ap()
    build(nc, *args, out)
    r = run_bass_kernel_spmd(nc, [arrays], core_ids=[0])
    return r.results[0]["out"]
```
